# Optimizing a Trainium2 kernel written in Bass

```python
import numpy as np
import jax
import jax.numpy as jnp

def _softmax(x, axis=-1):
    return jax.nn.softmax(x, axis=axis)
def _gelu(x):
    return jax.nn.gelu(x, approximate=True)
def _silu(x):
    return jax.nn.silu(x)
def _sigmoid(x):
    return jax.nn.sigmoid(x)
def _layernorm(x, axis=-1, eps=1e-5):
    m = jnp.mean(x, axis=axis, keepdims=True)
    v = jnp.var(x, axis=axis, keepdims=True)
    return (x - m) / jnp.sqrt(v + eps)
def _scatter_add(tgt, idx, src, axis=0):
    return tgt.at[idx].add(src)
def _segment_sum(src, seg, n):
    return jax.ops.segment_sum(src, seg, n)

kernel_name = 'mk_conv_preact_d4_conv_nhwc256_92dacc'

def setup_inputs(seed: int = 0):
    np.random.seed(seed)
    _w = jnp.asarray
    def _rec_inputs():
        import jax
        import jax.numpy as jnp
        _gk = jax.random.key(seed)
        x = 7.22e-05 + 1 * jax.random.normal(jax.random.fold_in(_gk, 1), (8, 64, 64, 256), jnp.float32)
        return x
    x = _rec_inputs()
    def _L0_conv_setup():
        import jax, jax.numpy as jnp
        import numpy as np
        B, H, W, C = (8, 64, 64, 256)
        G, K = (8, 3)
        GC = C // G
        K2 = K * K
        KD = 3
        OFFSET_SCALE = 1.0
        PAD = (K - 1) // 2
        EPS = 1e-06

        def _bilinear_gather(xg, px, py, Hp, Wp):
            x0 = jnp.floor(px)
            y0 = jnp.floor(py)
            wx1 = px - x0
            wy1 = py - y0
            x0i = x0.astype(jnp.int32)
            y0i = y0.astype(jnp.int32)

            def corner(xi, yi, wgt):
                valid = (xi >= 0) & (xi < Wp) & (yi >= 0) & (yi < Hp)
                idx = jnp.clip(yi, 0, Hp - 1) * Wp + jnp.clip(xi, 0, Wp - 1)
                v = jnp.take_along_axis(xg, idx[..., None], axis=2)
                return v * (wgt * valid)[..., None]
            return corner(x0i, y0i, (1 - wx1) * (1 - wy1)) + corner(x0i + 1, y0i, wx1 * (1 - wy1)) + corner(x0i, y0i + 1, (1 - wx1) * wy1) + corner(x0i + 1, y0i + 1, wx1 * wy1)
        key = jax.random.key(seed)
        ks = jax.random.split(key, 8)

        def r(k, shp, s):
            return jax.random.normal(k, shp, jnp.float32) * s
        return {'inputs': jax.random.normal(ks[0], (B, H, W, C), jnp.float32), 'w_in': r(ks[1], (C, C), 0.02), 'b_in': jnp.zeros((C,), jnp.float32), 'dw_kernel': r(ks[2], (KD, KD, 1, C), 0.1), 'dw_bias': jnp.zeros((C,), jnp.float32), 'ln_gamma': jnp.ones((C,), jnp.float32), 'ln_beta': jnp.zeros((C,), jnp.float32), 'w_off': r(ks[3], (C, 2 * G * K2), 0.01), 'b_off': jnp.zeros((2 * G * K2,), jnp.float32), 'w_mask': r(ks[4], (C, G * K2), 0.01), 'b_mask': jnp.zeros((G * K2,), jnp.float32), 'w_out': r(ks[5], (C, C), 0.02), 'b_out': jnp.zeros((C,), jnp.float32)}
    _L0_conv_all = _L0_conv_setup()
    _L0_conv_in = {k: v for k, v in _L0_conv_all.items() if k in ('w_in', 'b_in', 'dw_kernel', 'dw_bias', 'ln_gamma', 'ln_beta', 'w_off', 'b_off', 'w_mask', 'b_mask', 'w_out', 'b_out', )}
    del _L0_conv_all

    def _L1_conv_setup():
        import jax, jax.numpy as jnp
        import numpy as np

        def encode(x, embeddings):
            xf = x.reshape(-1, x.shape[-1])
            dis = jnp.sum(xf * xf, axis=-1, keepdims=True) + jnp.sum(embeddings * embeddings, axis=0, keepdims=True) - 2.0 * jnp.matmul(xf, embeddings)
            indices = jnp.argmin(dis, axis=-1)
            return indices.reshape(x.shape[:-1])

        def decode(indices, embeddings):
            return jnp.take(embeddings.T, indices, axis=0)
        key = jax.random.key(seed)
        k1, k2 = jax.random.split(key)
        B, H, W, D, K = (16, 64, 64, 256, 1024)
        x = jax.random.normal(k1, (B, H, W, D), dtype=jnp.float32)
        limit = np.sqrt(3.0 / D).astype(np.float32)
        embeddings = jax.random.uniform(k2, (D, K), dtype=jnp.float32, minval=-limit, maxval=limit)
        return {'x': x, 'embeddings': embeddings}
    _L1_conv_all = _L1_conv_setup()
    _L1_conv_in = {k: v for k, v in _L1_conv_all.items() if k in ('embeddings', )}
    del _L1_conv_all

    def _L2_conv_setup():
        import jax, jax.numpy as jnp
        import numpy as np
        HEADS = 8
        DIM_HEAD = 32
        SCALE = DIM_HEAD ** (-0.5)
        key = jax.random.key(seed)
        k1, k2, k3 = jax.random.split(key, 3)
        B, H, W, C = (16, 64, 64, 256)
        hidden = HEADS * DIM_HEAD
        x = jax.random.normal(k1, (B, H, W, C), dtype=jnp.float32)
        w_qkv = jax.random.normal(k2, (C, 3 * hidden), dtype=jnp.float32) * (1.0 / np.sqrt(C))
        w_out = jax.random.normal(k3, (hidden, C), dtype=jnp.float32) * (1.0 / np.sqrt(hidden))
        return {'x': x, 'w_qkv': w_qkv, 'w_out': w_out}
    _L2_conv_all = _L2_conv_setup()
    _L2_conv_in = {k: v for k, v in _L2_conv_all.items() if k in ('w_qkv', 'w_out', )}
    del _L2_conv_all

    def _L3_conv_setup():
        import jax, jax.numpy as jnp
        import numpy as np
        B, H, W, C = (16, 64, 64, 256)
        key = jax.random.key(seed)
        ks = jax.random.split(key, 4)
        x = jax.random.normal(ks[0], (B, H, W, C), dtype=jnp.float32)
        w1 = jax.random.normal(ks[1], (C,), dtype=jnp.float32) * C ** (-0.5)
        w2 = jax.random.normal(ks[2], (C,), dtype=jnp.float32) * C ** (-0.5)
        w3 = jax.random.normal(ks[3], (C,), dtype=jnp.float32) * C ** (-0.5)
        b1 = jnp.zeros((1,), jnp.float32)
        b2 = jnp.zeros((1,), jnp.float32)
        b3 = jnp.zeros((1,), jnp.float32)
        return {'x': x, 'w1': w1, 'b1': b1, 'w2': w2, 'b2': b2, 'w3': w3, 'b3': b3}
    _L3_conv_all = _L3_conv_setup()
    _L3_conv_in = {k: v for k, v in _L3_conv_all.items() if k in ('w1', 'b1', 'w2', 'b2', 'w3', 'b3', )}
    del _L3_conv_all

    return {
        "x": x,
        "L0_conv_w_in": _L0_conv_in["w_in"],
        "L0_conv_b_in": _L0_conv_in["b_in"],
        "L0_conv_dw_kernel": _L0_conv_in["dw_kernel"],
        "L0_conv_dw_bias": _L0_conv_in["dw_bias"],
        "L0_conv_ln_gamma": _L0_conv_in["ln_gamma"],
        "L0_conv_ln_beta": _L0_conv_in["ln_beta"],
        "L0_conv_w_off": _L0_conv_in["w_off"],
        "L0_conv_b_off": _L0_conv_in["b_off"],
        "L0_conv_w_mask": _L0_conv_in["w_mask"],
        "L0_conv_b_mask": _L0_conv_in["b_mask"],
        "L0_conv_w_out": _L0_conv_in["w_out"],
        "L0_conv_b_out": _L0_conv_in["b_out"],
        "L1_conv_embeddings": _L1_conv_in["embeddings"],
        "L2_conv_w_qkv": _L2_conv_in["w_qkv"],
        "L2_conv_w_out": _L2_conv_in["w_out"],
        "L3_conv_w1": _L3_conv_in["w1"],
        "L3_conv_b1": _L3_conv_in["b1"],
        "L3_conv_w2": _L3_conv_in["w2"],
        "L3_conv_b2": _L3_conv_in["b2"],
        "L3_conv_w3": _L3_conv_in["w3"],
        "L3_conv_b3": _L3_conv_in["b3"],
    }

def reference(x, L0_conv_w_in, L0_conv_b_in, L0_conv_dw_kernel, L0_conv_dw_bias, L0_conv_ln_gamma, L0_conv_ln_beta, L0_conv_w_off, L0_conv_b_off, L0_conv_w_mask, L0_conv_b_mask, L0_conv_w_out, L0_conv_b_out, L1_conv_embeddings, L2_conv_w_qkv, L2_conv_w_out, L3_conv_w1, L3_conv_b1, L3_conv_w2, L3_conv_b2, L3_conv_w3, L3_conv_b3):
    import jax
    import jax.numpy as jnp
    def _L0_conv_ref(inputs, w_in, b_in, dw_kernel, dw_bias, ln_gamma, ln_beta, w_off, b_off, w_mask, b_mask, w_out, b_out):
        import jax, jax.numpy as jnp
        import numpy as np
        B, H, W, C = (8, 64, 64, 256)
        G, K = (8, 3)
        GC = C // G
        K2 = K * K
        KD = 3
        OFFSET_SCALE = 1.0
        PAD = (K - 1) // 2
        EPS = 1e-06

        def _bilinear_gather(xg, px, py, Hp, Wp):
            x0 = jnp.floor(px)
            y0 = jnp.floor(py)
            wx1 = px - x0
            wy1 = py - y0
            x0i = x0.astype(jnp.int32)
            y0i = y0.astype(jnp.int32)

            def corner(xi, yi, wgt):
                valid = (xi >= 0) & (xi < Wp) & (yi >= 0) & (yi < Hp)
                idx = jnp.clip(yi, 0, Hp - 1) * Wp + jnp.clip(xi, 0, Wp - 1)
                v = jnp.take_along_axis(xg, idx[..., None], axis=2)
                return v * (wgt * valid)[..., None]
            return corner(x0i, y0i, (1 - wx1) * (1 - wy1)) + corner(x0i + 1, y0i, wx1 * (1 - wy1)) + corner(x0i, y0i + 1, (1 - wx1) * wy1) + corner(x0i + 1, y0i + 1, wx1 * wy1)
        x_proj = inputs @ w_in + b_in
        x1 = jax.lax.conv_general_dilated(inputs, dw_kernel, (1, 1), 'SAME', dimension_numbers=('NHWC', 'HWIO', 'NHWC'), feature_group_count=C) + dw_bias
        mu = jnp.mean(x1, -1, keepdims=True)
        var = jnp.mean(jnp.square(x1 - mu), -1, keepdims=True)
        x1 = (x1 - mu) * jax.lax.rsqrt(var + EPS) * ln_gamma + ln_beta
        x1 = jax.nn.gelu(x1, approximate=False)
        offset = (x1 @ w_off + b_off).reshape(B, H, W, G, K2, 2)
        mask = jax.nn.softmax((x1 @ w_mask + b_mask).reshape(B, H, W, G, K2), axis=-1)
        ky, kx = jnp.meshgrid(jnp.arange(K) - PAD, jnp.arange(K) - PAD, indexing='ij')
        kx = kx.reshape(-1).astype(jnp.float32)
        ky = ky.reshape(-1).astype(jnp.float32)
        px = (PAD + jnp.arange(W, dtype=jnp.float32))[None, None, :, None, None] + (kx + offset[..., 0]) * OFFSET_SCALE
        py = (PAD + jnp.arange(H, dtype=jnp.float32))[None, :, None, None, None] + (ky + offset[..., 1]) * OFFSET_SCALE
        Hp, Wp = (H + 2 * PAD, W + 2 * PAD)
        x_pad = jnp.pad(x_proj, ((0, 0), (PAD, PAD), (PAD, PAD), (0, 0)))
        xg = x_pad.reshape(B, Hp * Wp, G, GC).transpose(0, 2, 1, 3)
        N = H * W * K2
        pxf = px.transpose(0, 3, 1, 2, 4).reshape(B, G, N)
        pyf = py.transpose(0, 3, 1, 2, 4).reshape(B, G, N)
        samp = _bilinear_gather(xg, pxf, pyf, Hp, Wp).reshape(B, G, H, W, K2, GC)
        maskg = mask.transpose(0, 3, 1, 2, 4)
        out = jnp.sum(samp * maskg[..., None], axis=4)
        out = out.transpose(0, 2, 3, 1, 4).reshape(B, H, W, C)
        return out @ w_out + b_out

    def _L1_conv_ref(x, embeddings):
        import jax, jax.numpy as jnp
        import numpy as np

        def encode(x, embeddings):
            xf = x.reshape(-1, x.shape[-1])
            dis = jnp.sum(xf * xf, axis=-1, keepdims=True) + jnp.sum(embeddings * embeddings, axis=0, keepdims=True) - 2.0 * jnp.matmul(xf, embeddings)
            indices = jnp.argmin(dis, axis=-1)
            return indices.reshape(x.shape[:-1])

        def decode(indices, embeddings):
            return jnp.take(embeddings.T, indices, axis=0)
        indices = encode(x, embeddings)
        quantized = decode(indices, embeddings)
        return quantized

    def _L2_conv_ref(x, w_qkv, w_out):
        import jax, jax.numpy as jnp
        import numpy as np
        HEADS = 8
        DIM_HEAD = 32
        SCALE = DIM_HEAD ** (-0.5)
        B, H, W, C = x.shape
        n = H * W
        qkv = jnp.einsum('bhwc,cf->bhwf', x, w_qkv)
        q, k, v = jnp.split(qkv, 3, axis=-1)

        def to_heads(t):
            t = t.reshape(B, n, HEADS, DIM_HEAD)
            return jnp.transpose(t, (0, 2, 3, 1))
        q, k, v = (to_heads(q), to_heads(k), to_heads(v))
        q = jax.nn.softmax(q, axis=-2) * SCALE
        k = jax.nn.softmax(k, axis=-1)
        context = jnp.einsum('bhdn,bhen->bhde', k, v)
        out = jnp.einsum('bhde,bhdn->bhen', context, q)
        out = jnp.transpose(out, (0, 3, 1, 2)).reshape(B, H, W, HEADS * DIM_HEAD)
        return jnp.einsum('bhwf,fc->bhwc', out, w_out)

    def _L3_conv_ref(x, w1, b1, w2, b2, w3, b3):
        import jax, jax.numpy as jnp
        import numpy as np
        B, H, W, C = (16, 64, 64, 256)
        b, h, w, c = x.shape
        n = h * w
        xf = x.reshape(b, n, c)
        x0 = jnp.einsum('bnc,c->bn', xf, w1) + b1[0]
        x1 = jnp.einsum('bnc,c->bn', xf, w2) + b2[0]
        x2 = jnp.einsum('bnc,c->bn', xf, w3) + b3[0]
        sim = x0[:, :, None] * x1[:, None, :]
        sm = jax.nn.softmax(sim, axis=1)
        feats = jnp.einsum('bn,bnm->bm', x2, sm)
        gate = jax.nn.sigmoid(feats).reshape(b, h, w, 1)
        return gate * x

    def _gn(v, G=32, eps=1e-5):
        B_, H_, W_, C_ = v.shape
        g = v.reshape(B_, H_, W_, G, C_ // G)
        m = jnp.mean(g, axis=(1, 2, 4), keepdims=True)
        s = jnp.var(g, axis=(1, 2, 4), keepdims=True)
        return ((g - m) / jnp.sqrt(s + eps)).reshape(v.shape)

    def _ln_c(v, eps=1e-6):
        m = jnp.mean(v, axis=-1, keepdims=True)
        s = jnp.var(v, axis=-1, keepdims=True)
        return (v - m) / jnp.sqrt(s + eps)

    def _ln_t(v, eps=1e-5):
        m = jnp.mean(v, axis=-1, keepdims=True)
        s = jnp.var(v, axis=-1, keepdims=True)
        return (v - m) / jnp.sqrt(s + eps)

    def _to_tokens(v):
        B_, H_, W_, C_ = v.shape
        return v.reshape(B_, H_ * W_, C_)
    def _from_tokens(t, like):
        return t.reshape(like.shape)

    x = x + _L0_conv_ref(_gn(x), L0_conv_w_in, L0_conv_b_in, L0_conv_dw_kernel, L0_conv_dw_bias, L0_conv_ln_gamma, L0_conv_ln_beta, L0_conv_w_off, L0_conv_b_off, L0_conv_w_mask, L0_conv_b_mask, L0_conv_w_out, L0_conv_b_out)
    x = x + _L1_conv_ref(_gn(x), L1_conv_embeddings)
    x = x + _L2_conv_ref(_gn(x), L2_conv_w_qkv, L2_conv_w_out)
    x = x + _L3_conv_ref(_gn(x), L3_conv_w1, L3_conv_b1, L3_conv_w2, L3_conv_b2, L3_conv_w3, L3_conv_b3)
    return x


_drawn_inputs = setup_inputs


def setup_inputs(seed=0):
    import zlib

    import numpy as np

    out = dict(_drawn_inputs(seed))
    spreads = {'L0_conv_b_in': (0.0, 0.1),
     'L0_conv_dw_bias': (0.0, 0.8),
     'L0_conv_ln_gamma': (1.0, 0.6),
     'L0_conv_ln_beta': (0.0, 0.8),
     'L0_conv_b_off': (0.0, 0.8),
     'L0_conv_b_out': (0.0, 0.1)}
    factors = {'L0_conv_dw_kernel': 6.514,
     'L0_conv_w_off': 6.504,
     'L2_conv_w_qkv': 3.699,
     'L2_conv_w_out': 4.099,
     'L3_conv_w1': 7.092,
     'L3_conv_w2': 5.387}
    for name, (base, spread) in spreads.items():
        noise = np.random.default_rng([zlib.crc32(name.encode()), seed]).standard_normal(out[name].shape)
        drawn = base * np.exp(spread * noise) if base else spread * noise
        out[name] = jnp.asarray(drawn.astype(out[name].dtype))
    for name, factor in factors.items():
        out[name] = (out[name] * factor).astype(out[name].dtype)
    return out
```

```python
from contextlib import ExitStack

import numpy as np

import concourse.bass as bass
from concourse import mybir

ALU = mybir.AluOpType
ACT = mybir.ActivationFunctionType
AX = mybir.AxisListType
F32 = mybir.dt.float32
I32 = mybir.dt.int32
U32 = mybir.dt.uint32

P = 128
B, H, W, C = 8, 64, 64, 256
N = H * W
CH = C // P
G, K2 = 8, 9
GC = C // G
GK = G * K2
NOFF = 2 * GK
NPROJ = NOFF + GK
TILES = N // P
CHUNK = 512
CHUNKS = N // CHUNK
QT = CHUNK // P
ROWS = CHUNK // W
PITCH = W + 2
PROWS = H + 3
ENTRIES = 34
ESPAN = P + PITCH + 2
QUAD = 4 * GC
CODES = 1024
CB = CODES // P
HEADS, DH = 8, 32
GROUP = 8
MAGIC = 12582912.0

COLS = {}
_at = 0
for _name, _n in (("ident", P), ("group", P), ("heads", P), ("ones", P), ("valid", ENTRIES * 4),
                  ("base", NOFF),
                  ("trow", TILES), ("gidx", GK), ("code", CB), ("mhalf", 1)):
    COLS[_name] = slice(_at, _at + _n)
    _at += _n
NCONST = _at


def constants():
    c = np.zeros((P, NCONST), np.float32)
    p = np.arange(P)
    c[:, COLS["ident"]] = np.eye(P)
    c[:, COLS["group"]] = (p[:, None] // GROUP == p[None] // GROUP) / GROUP
    c[:, COLS["heads"]] = p[:, None] // DH == p[None] // DH
    c[:, COLS["ones"]] = 1
    e = np.arange(ENTRIES)[None, :, None] * P + p[:, None, None]
    q = e + np.array([0, 1, PITCH, PITCH + 1])[None, None]
    row, col = q // PITCH, q % PITCH
    c[:, COLS["valid"]] = ((row >= 1) & (row <= H) & (col >= 1) & (col <= W)).reshape(P, -1)
    ky, kx = np.meshgrid(np.arange(3) - 1, np.arange(3) - 1, indexing="ij")
    base = np.stack([1 + (p % W)[:, None] + kx.reshape(1, -1), 1 + (p // W)[:, None] + ky.reshape(1, -1)], -1)
    c[:, COLS["base"]] = np.broadcast_to(base[:, None], (P, G, K2, 2)).reshape(P, -1)
    c[:, COLS["trow"]] = np.arange(TILES)[None] * (P // W)
    c[:, COLS["gidx"]] = np.repeat(np.arange(G), K2)[None]
    c[:, COLS["code"]] = p[:, None] + np.arange(CB)[None] * P
    c[:, COLS["mhalf"]] = -0.5
    return c


class Steps:

    def __init__(self, unit, per):
        self.before, self.per, self.n = unit * per, per, 0

    def next(self):
        self.n += 1
        assert self.n <= self.per
        return self.before + self.n

    def end(self):
        assert self.n == self.per, (self.n, self.per)


W_STEPS, CONV_STEPS, LN_STEPS, NORM_STEPS, VQ_STEPS, Q_STEPS, A_STEPS, X_STEPS = 18, 2 * K2, 9, 8, 3, 3, 4, 6
SPLIT = 6
LOADS = 16 * 15
EPS_GN, EPS_LN = 1e-5, 1e-6


def build(nc, t, out):
    ctx = ExitStack()

    def sb(name, shape, dt=F32):
        return ctx.enter_context(nc.sbuf_tensor(name, shape, dt))

    def pb(name, shape):
        return ctx.enter_context(nc.psum_tensor(name, shape, F32))

    def sem(name):
        return ctx.enter_context(nc.semaphore(name))

    def at(k, n=P):
        return bass.ds(k, n)

    with ctx:
        tables = [nc.dram_tensor(f"table{i}", (ENTRIES * P * G, QUAD), F32, kind="Internal").ap() for i in range(2)]
        offs_d = nc.dram_tensor("offsets", (B * TILES, P, NPROJ), F32, kind="Internal").ap()
        x1_d = nc.dram_tensor("x1", (B, CH, P, N), F32, kind="Internal").ap()
        x2_d = nc.dram_tensor("x2", (B, CH, P, N), F32, kind="Internal").ap()
        x3_d = nc.dram_tensor("x3", (B, CH, P, N), F32, kind="Internal").ap()
        e2_d = nc.dram_tensor("e2", (1, CODES), F32, kind="Internal").ap()

        cst = sb("cst", [P, NCONST])

        def const(name):
            return cst[:, COLS[name]]

        ident, ones_m, group_m, valid, code = (const(k) for k in ("ident", "ones", "group", "valid", "code"))
        w_in = sb("w_in", [P, CH, C])
        w_om = sb("w_om", [P, CH, NPROJ])
        w_o0 = sb("w_o0", [P, CH, C])
        wx = sb("wx", [P, 2048])
        w_qkv = wx[:, 0:CH * 3 * C].rearrange("p (h n) -> p h n", h=CH)
        ex = wx[:, :].rearrange("p (s n) -> p s n", s=2)
        w_o2 = sb("w_o2", [P, CH, C])
        dwk = sb("dwk", [P, CH, K2])
        cols = sb("cols", [P, 7, CH])
        w3 = cols[:, 4:7, :]
        w13 = sb("w13", [P, 2, CH, P])
        b3 = sb("b3", [P, 3])
        bin_bc = sb("bin_bc", [P, C])
        om_bc = sb("om_bc", [P, NPROJ])
        kmrow = sb("kmrow", [1, 2 * C])
        pad = sb("pad", [P, CH, PROWS, PITCH])
        padf = pad[:, :, :, :].rearrange("p h r c -> p h (r c)")
        fstat = sb("fstat", [P, CH, CHUNKS, 6])
        stg = sb("stg", [P, CH, ESPAN])
        R2 = sb("R2", [P, 2, 1024])
        xf = R2[:, :, :].rearrange("p s (h n) -> p s h n", h=CH)
        tabt = R2[:, :, :].rearrange("p s (g a c) -> p s g a c", g=G, a=4)
        cv = R2[:, 0, :].rearrange("p (h n) -> p h n", h=CH)
        ge = cv
        ln = R2[:, 1, :].rearrange("p (q c) -> p q c", q=QT)
        osb = R2[:, 1, 0:QT * NPROJ]
        ls6 = sb("ls6", [P, QT, 6])
        lmv = sb("lmv", [P, QT, 2])
        lsd = sb("lsd", [P, 4, QT])
        gath = sb("gath", [P, 2, GK, QUAD])
        idx = sb("idx", [P, 2, GK], I32)
        wts = sb("wts", [P, 2, GK, 4])
        of = sb("of", [P, 2, NPROJ])
        pos = sb("pos", [P, GK, 2])
        rnd = sb("rnd", [P, GK, 2])
        hat = sb("hat", [P, 2, GK, 2])
        wy = sb("wy", [P, 2, GK])
        lb = sb("lb", [P, 3, GK])
        lg = sb("lg", [P, 3, G])
        ib = sb("ib", [P, GK])
        samp = sb("samp", [P, C])
        sT = sb("sT", [P, CH, P])
        xr = sb("xr", [P, CH, P])
        x1t = sb("x1t", [P, CH, P])
        st1 = sb("st1", [P, CH, TILES, 6])
        xp = sb("xp", [P, 2, CH, CHUNK])
        R3 = sb("R3", [P, 1280])
        gn = R3[:, 0:CH * CHUNK].rearrange("p (h n) -> p h n", h=CH)
        gt = R3[:, 0:C].rearrange("p (h n) -> p h n", h=CH)
        sq = R3[:, C:2 * C].rearrange("p (h n) -> p h n", h=CH)
        ke, vv = R3[:, C:2 * C], R3[:, 2 * C:3 * C]
        qe, qn = R3[:, 3 * C:4 * C], R3[:, 4 * C:5 * C]
        xs, outt = R3[:, C:2 * C], R3[:, 2 * C:3 * C]
        big = sb("big", [P, 8192])
        emb = big[:, 0:2048].rearrange("p (h k) -> p h k", h=CH)
        embT = big[:, 2048:4096].rearrange("p (k c) -> p k c", k=CB)
        sc = big[:, 4096:6144].rearrange("p (s k) -> p s k", s=2)
        hot = big[:, 6144:7168].rearrange("p (k n) -> p k n", k=CB)
        qT = big[:, :].rearrange("p (h n) -> p h n", h=CH)
        x02 = qT
        e2row = big[0:1, 7168:8192]
        m8 = sb("m8", [P, 8])
        i8 = sb("i8", [P, 8], U32)
        x2c, idf = sb("x2c", [P, 1]), sb("idf", [P, 1])
        kmx, qmx, qsm = sb("kmx", [P, CH]), sb("qmx", [P, HEADS]), sb("qsm", [P, HEADS])
        rden = sb("rden", [P, CH])
        dn, dn2 = sb("dn", [P, 2, 4]), sb("dn2", [P, 2])
        rec, feat, gex, gate = (sb(k, [P, 1]) for k in ("rec", "feat", "gex", "gate"))
        gate1 = sb("gate1", [P, 1])
        xmm = sb("xmm", [P, 2])
        dg = R3[:, 2 * C:2 * C + P]
        km = sb("km", [P, CH, CHUNKS])
        ctxa = sb("ctxa", [P, CH, P + 1])
        cm = gt
        M = sb("M", [P, CH, C])
        xmn = sb("xmn", [P, 2, CHUNKS])
        x1c = sb("x1c", [P, TILES])
        nb = sb("nb", [P, 3, TILES])
        stp = sb("stp", [P, CH, CHUNKS, 6])
        nrm = {k: sb(f"nrm{k}", [P, 10, CH]) for k in "FP"}

        psF = pb("psF", [P, 2, 512])
        psF4 = psF[:, :, :].rearrange("p b (a c) -> p (b a) c", c=C)
        psP = pb("psP", [P, 2, 512])
        psPf = psP[:, :, :].rearrange("p b n -> p (b n)")
        psS = pb("psS", [P, 2, CH, P])
        psO = pb("psO", [P, 2, 512])
        psM = pb("psM", [P, 512])

        CREDITS = {
            "sync": {},
            "vector": {"f_stat": 1, "tab_evac": 1, "of_used": 2, "samp_ready": 2, "x1_ready": 1, "big_free": 1,
                       "vq_diag": 2, "km_red": 1, "q_sub": 1, "q_acc": 1, "o_upd": 1, "l_red": 1, "a_ttr": 2,
                       "a_out": 1, "xp_rel": 2, "tab_free": 2, "x1_free": 1, "off_stored": 1, "out_free": 1},
            "scalar": {"f_applied": 1, "vq_sc": 1, "q_ev": 1, "q_T": 1, "l_ev": 1},
            "tensor": {"proj": 1, "tab_mm": 1, "vq_mm": 1, "km_mm": 1, "q_mm": 1, "q_ctx": 1, "l_mm": 1},
        }
        names = """held in_parts e2st setup_dve setup_pe setup_act
            f_loadA f_loadB f_stat f_applied conv_own cvT ln_own ln_var ln_root ln_scale ln_done lnT gelu proj
            osb offst off_stored staged tab_mm tab_evac tab0 tab1 tab_free
            of0 of1 of_used lm mexp w_own idx_ready gath00 gath01 gath10 gath11 c_own samp_ready sampT sT_ready so
            x1_ready x1st xr_ld x1_free st1_done
            emb_ld big_free xp0 xp1 xp_rel xst st_done
            vq_gt vq_sq vq_mm vq_x2 vq_sc vq_own vq_diag vq_bc vq_hot vq_q vq_upd
            km_gn km_mm km_red km_own km_row km_rowc
            q_gt q_mm q_own q_sub q_ev q_exp q_n q_ctx q_acc q_tr q_T
            m_own m_mm m_done o_mm o_upd l_gn l_mm l_red l_ev x_own
            a_x a_ttr a_own a_gt a_feat a_gex a_tr a_xs a_out outst out_free
            nF_d nF_p nF_a nF_done nP_d nP_p nP_a nP_done""".split()
        S = {n: sem(n) for n in names}
        block = ctx.enter_context(nc.Block())

        def hold(eng):
            eng.sem_inc(S["held"], 1)

        def schedule(eng, w, period=1):
            def do(name, *a):
                if name in w:
                    w[name](*a)

            def steps(b, first, count, beside, sampling, image_end=False, last=False):
                def pair(i, wrap):
                    for par in range(2):
                        s = i * 2 + par
                        beside(s, par, i)
                        if sampling:
                            n, half = b * TILES + first + s, b * (TILES // 2) + first // 2 + i
                            if not (wrap and par):
                                do("weights", n + 1, 1 - par, half + par, b, first + s + 1)
                            elif not last:
                                do("weights", n + 1, 0, half + 1, b + 1, 0)
                            part = int(first >= SPLIT * 2)
                            do("consume", n, par, part, first // 2 - SPLIT * part + i, b, first + s)

                turns = count // 2
                if sampling and image_end:
                    with eng.Fori(0, turns - 1) as i:
                        pair(i, False)
                    pair(turns - 1, True)
                elif turns == 1:
                    pair(0, False)
                else:
                    with eng.Fori(0, turns) as i:
                        pair(i, False)

            def image(b, sampling, post, front, odd=0):
                pi, fi = b - 1, b + 1

                def beside_vq(s, par, i):
                    if post:
                        do("vq", pi, s, par, i)
                    if front:
                        do("f_stats", fi * CHUNKS + s, fi, s)

                def beside_kmax(s, par, i):
                    for q in range(2):
                        if post:
                            do("kmax", pi, s * 2 + q, q, s)
                        if front:
                            do("f_apply", fi * CHUNKS + s * 2 + q, fi, s * 2 + q)

                def beside_qkv(s, par, i):
                    for q in range(QT):
                        if post:
                            do("qkv_a", pi, s, q, par, i)
                        if front:
                            do("entries", fi, s * QT + q, s * 2 + q // 2, q % 2, 1 - odd)
                        if post:
                            do("qkv_b", pi, s, q, par)

                def beside_out(s, par, i):
                    for q in range(4):
                        if post:
                            do("out", pi, s * 4 + q, q % 2, s * 2 + q // 2)

                def beside_pre(s, par, i):
                    for q in range(4):
                        if post:
                            do("pre", pi, s * 4 + q, q % 2, s * 2 + q // 2)

                def beside_att(s, par, i):
                    for q in range(QT):
                        if post:
                            do("att", pi, s, q, par, i)
                        if front and q:
                            do(("", "ln_a", "ln_b", "ln_c")[q], fi, s)

                if post:
                    do("post_start", pi)
                    do("norm", "P", pi * 3, st1, "st1_done", (pi + 1) * 2 * TILES)
                steps(b, 0, 8, beside_vq, sampling)
                if post:
                    do("norm", "P", pi * 3 + 1, stp, "st_done", pi * 32 + 16)
                if front:
                    do("norm", "F", fi, fstat, "f_stat", (fi + 1) * CHUNKS + 1)
                steps(b, 8, 4, beside_kmax, sampling)
                if post:
                    do("kmax_end", pi)
                steps(b, 12, 8, beside_qkv, sampling)
                if post:
                    do("ctx_end", pi)
                if front:
                    for q in range(ENTRIES - TILES):
                        do("entries", fi, TILES + q, TILES // 2, q, 1 - odd)
                steps(b, 20, 2, beside_out, sampling)
                if post:
                    do("norm", "P", pi * 3 + 2, stp, "st_done", pi * 32 + 32)
                steps(b, 22, 2, beside_pre, sampling)
                if post:
                    do("pre_end", pi)
                steps(b, 24, 8, beside_att, sampling, image_end=True, last=not front)
                if post:
                    do("post_end", pi)

            do("setup")
            image(-1, sampling=False, post=False, front=True, odd=1)
            do("weights", 0, 0, 0, 0, 0)
            image(0, sampling=True, post=False, front=True)
            with eng.Fori(0, (B - 2) // period) as i:
                for k in range(period):
                    image(i * period + (1 + k), sampling=True, post=True, front=True, odd=1 - k)
            image(B - 1, sampling=True, post=True, front=False)
            image(B, sampling=False, post=True, front=False)

        def credit(eng, name):
            for k, v in CREDITS[name].items():
                eng.sem_inc(S[k], v)

        @block.sync
        def _(sp):
            def halves(dram, b, k, n):
                return dram[at(b, 1), :, :, at(k, n)].rearrange("b h p n -> p (b h) n")

            def setup():
                def ld(dst, src):
                    sp.dma_start(dst, src).then_inc(S["in_parts"], 16)

                ld(cst[:, :], t["consts"])
                for dst, name in ((w_in, "w_in"), (w_o0, "w_out0"), (w_o2, "w_out2"), (dwk, "dwk")):
                    ld(dst[:, :, :], t[name].rearrange("(h p) n -> p h n", p=P))
                ld(w_om[:, :, 0:NOFF], t["w_off"].rearrange("(h p) n -> p h n", p=P))
                ld(w_om[:, :, NOFF:NPROJ], t["w_mask"].rearrange("(h p) n -> p h n", p=P))
                ld(cols[:, :, :], t["cols"])
                for i in range(3):
                    ld(b3[:, i:i + 1], t[f"b{i + 1}"].partition_broadcast(P))
                ld(bin_bc[:, :], t["b_in"].partition_broadcast(P))
                ld(om_bc[:, 0:NOFF], t["b_off"].partition_broadcast(P))
                ld(om_bc[:, NOFF:NPROJ], t["b_mask"].partition_broadcast(P))
                ld(emb, t["emb"].rearrange("(h p) k -> p h k", p=P))
                sp.wait_ge(S["setup_act"], 2)
                sp.dma_start(e2_d, e2row).then_inc(S["e2st"], 16)
                sp.wait_ge(S["e2st"], 16)

            def chunk_in(pi, stage, c, slot, src):
                sp.wait_ge(S["xp_rel"], pi * 48 + stage * 8 + c + 1)
                hold(sp)
                sp.dma_start(xp[:, slot, :, :], halves(src, pi, c * CHUNK, CHUNK)).then_inc(S[f"xp{slot}"], 16)

            def chunk_out(pi, c, slot, dst, stage):
                sp.wait_ge(S["st_done"], pi * 32 + stage * 16 + (c + 1) * 2)
                hold(sp)
                sp.dma_start(halves(dst, pi, c * CHUNK, CHUNK), xp[:, slot, :, :]).then_inc(S["xst"], 16)
                sp.wait_ge(S["xst"], (pi * 16 + stage * 8 + c + 1) * 16)
                sp.sem_inc(S["xp_rel"], 1)

            def post_start(pi):
                sp.wait_ge(S["big_free"], pi + 1)
                sp.dma_start(emb, t["emb"].rearrange("(h p) k -> p h k", p=P)).then_inc(S["emb_ld"], 16)
                sp.dma_start(embT, t["embT"].rearrange("(k p) c -> p k c", p=P)).then_inc(S["emb_ld"], 16)
                sp.dma_start(e2row, e2_d).then_inc(S["emb_ld"], 16)
                sp.dma_start(w_qkv, t["w_qkv"].rearrange("(h p) n -> p h n", p=P)).then_inc(S["emb_ld"], 16)

            def vq(pi, s, par, i):
                chunk_in(pi, 0, s, par, x1_d)
                chunk_out(pi, s, par, x2_d, 0)

            def kmax(pi, c, slot, hc):
                chunk_in(pi, 1, c, slot, x2_d)

            def qkv_a(pi, s, q, par, i):
                if q == 0:
                    chunk_in(pi, 2, s, par, x2_d)

            def outp(pi, c, slot, hc):
                chunk_in(pi, 3, c, slot, x2_d)
                chunk_out(pi, c, slot, x3_d, 1)

            def pre(pi, c, slot, hc):
                chunk_in(pi, 4, c, slot, x3_d)

            def att(pi, s, q, par, i):
                m = (pi * CHUNKS + s) * QT + q
                if q == 0:
                    chunk_in(pi, 5, s, par, x3_d)
                sp.wait_ge(S["a_out"], m + 2)
                sp.dma_start(out[at(pi, 1), at(s * CHUNK + q * P), :].rearrange("b p c -> p (b c)"), outt)\
                    .then_inc(S["outst"], 16)
                sp.wait_ge(S["outst"], (m + 1) * 16)
                sp.sem_inc(S["out_free"], 1)

            def f_stats(c, fi, s):
                sp.wait_ge(S["f_stat"], c + 1)
                sp.dma_start(xf[:, 0, :, :], halves(t["xT"], fi, s * CHUNK, CHUNK)).then_inc(S["f_loadA"], 16)

            def f_apply(c, fi, s):
                sp.wait_ge(S["f_applied"], c + 1)
                sp.dma_start(xf[:, 1, :, :], halves(t["xT"], fi, s * CHUNK, CHUNK)).then_inc(S["f_loadB"], 16)

            def entries(fi, et, half, slot, odd):
                e = fi * ENTRIES + et
                sp.wait_ge(S["tab_evac"], e + 2)
                table = tables[odd].rearrange("(e p g) q -> e p (g q)", p=P, g=G)
                sp.dma_start(table[at(et, 1), :, :].rearrange("e p q -> p (e q)"), R2[:, slot, :])\
                    .then_inc(S[f"tab{slot}"], 16)
                sp.wait_ge(S[f"tab{slot}"], (fi * (ENTRIES // 2) + half + 1) * 16)
                sp.sem_inc(S["tab_free"], 1)

            def ln_c(fi, s):
                c = fi * CHUNKS + s
                sp.wait_ge(S["osb"], c + 1)
                sp.dma_start(offs_d[at(c * QT, QT), :, :].rearrange("q p n -> p q n"),
                             osb.rearrange("p (q n) -> p q n", q=QT)).then_inc(S["offst"], 16)
                sp.wait_ge(S["offst"], (c + 1) * 16)
                sp.sem_inc(S["off_stored"], 1)

            def weights(n, slot, half, b, tile):
                sp.wait_ge(S["of_used"], n + 1)
                sp.dma_start(of[:, slot, :], offs_d[at(n, 1), :, :].rearrange("o p n -> p (o n)"))\
                    .then_inc(S[f"of{slot}"], 16)

            def consume(n, slot, part, half, b, tile):
                sp.wait_ge(S["x1_ready"], n + 1)
                sp.dma_start(xr[:, :, :], halves(t["xT"], b, tile * P, P)).then_inc(S["xr_ld"], 16)
                sp.wait_ge(S["x1_ready"], n + 2)
                sp.dma_start(halves(x1_d, b, tile * P, P), x1t[:, :, :]).then_inc(S["x1st"], 16)
                sp.wait_ge(S["x1st"], (n + 1) * 16)
                sp.sem_inc(S["x1_free"], 1)

            schedule(sp, dict(setup=setup, post_start=post_start, vq=vq, kmax=kmax, qkv_a=qkv_a, out=outp, pre=pre,
                              att=att, f_stats=f_stats, f_apply=f_apply, entries=entries, ln_c=ln_c,
                              weights=weights, consume=consume), period=2)

        @block.gpsimd
        def _(pool):
            def pair(b, part, i, table):
                for slot in range(2):
                    n = b * TILES + (SPLIT * part + i) * 2 + slot
                    pool.wait_ge(S["idx_ready"], n + 1)
                    pool.wait_ge(S["samp_ready"], n + 1)
                    hold(pool)
                    for k in range(GK):
                        pool.indirect_dma_start(
                            gath[:, slot, k, :], None, table[:, :],
                            bass.IndirectOffsetOnAxis(ap=idx[:, slot, k:k + 1].bitcast(U32), axis=0))\
                            .then_inc(S[f"gath{part}{slot}"], 16)

            def lower(part, n):
                pool.wait_ge(S["samp_ready"], n + 2)
                hold(pool)
                pairs = (SPLIT, TILES // 2 - SPLIT)[part]
                pool.inc_swdge_sem([S[f"gath{part}{slot}"] for slot in range(2)], [pairs * GK * 16] * 2, mode="sub")

            def image(b, odd, first=False):
                for slot in range(2):
                    pool.wait_ge(S[f"tab{slot}"], (b + 1) * (ENTRIES // 2 * 16))
                hold(pool)
                for part, pairs in enumerate((SPLIT, TILES // 2 - SPLIT)):
                    pair(b, part, 0, tables[odd])
                    if part or not first:
                        lower(1 - part, b * TILES + SPLIT * 2 * part)
                    with pool.Fori(1, pairs) as i:
                        pair(b, part, i, tables[odd])

            image(0, 0, first=True)
            with pool.Fori(0, (B - 2) // 2) as i:
                for k in range(2):
                    image(i * 2 + (1 + k), 1 - k)
            image(B - 1, 1)

        @block.scalar
        def _(act):
            def setup():
                credit(act, "scalar")
                act.wait_ge(S["in_parts"], LOADS)
                act.activation(sc, emb, ACT.Square).then_inc(S["setup_act"], 1)
                act.wait_ge(S["setup_pe"], 1)
                act.activation(e2row, psPf[0:1, :], ACT.Copy).then_inc(S["setup_act"], 1)
                act.wait_ge(S["setup_dve"], SETUP_DVE)

            def affine(dst, src, kind):
                for h in range(CH):
                    last = act.activation(dst(h), src(h), ACT.Identity, bias=nrm[kind][:, 9, h:h + 1],
                                          scale=nrm[kind][:, 8, h:h + 1])
                return last

            def norm(kind, j, st, ready, value):
                act.wait_ge(S[f"n{kind}_d"], j * NORM_STEPS + 7)
                act.activation(nrm[kind][:, 6, :], nrm[kind][:, 5, :], ACT.Sqrt).then_inc(S[f"n{kind}_a"], 1)

            def vq(pi, s, par, i):
                m0 = (pi * CHUNKS + s) * QT

                def normed(q):
                    m = m0 + q
                    act.wait_ge(S["vq_mm"], m + 1)
                    affine(lambda h: gt[:, h, :], lambda h: xp[:, par, h, q * P:(q + 1) * P], "P")\
                        .then_inc(S["vq_gt"], 1)
                    act.wait_ge(S["vq_gt"], m + 1)
                    act.activation(sq, gt, ACT.Square).then_inc(S["vq_sq"], 1)

                def scored(q):
                    m = m0 + q
                    act.wait_ge(S["vq_mm"], m + 2)
                    act.activation(x2c[:, :], psO[:, 1, 0:1], ACT.Copy).then_inc(S["vq_x2"], 1)
                    act.wait_ge(S["vq_x2"], m + 1)
                    act.wait_ge(S["vq_diag"], m + 1)
                    act.activation(sc[:, q % 2, :], psPf, ACT.Identity, bias=x2c[:, :]).then_inc(S["vq_sc"], 1)

                act.wait_ge(S["nP_done"], pi * 3 + 1)
                act.wait_ge(S[f"xp{par}"], (pi * 24 + i + 1) * 16)
                for q in range(QT):
                    normed(q)
                    scored(q)

            def kmax(pi, c, slot, hc):
                k = pi * CHUNKS + c
                act.wait_ge(S["nP_done"], pi * 3 + 2)
                act.wait_ge(S[f"xp{slot}"], (pi * 24 + 4 + hc + 1) * 16)
                act.wait_ge(S["km_mm"], k + 1)
                affine(lambda h: gn[:, h, :], lambda h: xp[:, slot, h, :], "P").then_inc(S["km_gn"], 1)
                act.wait_ge(S["km_gn"], k + 1)
                act.sem_inc(S["xp_rel"], 1)

            def kmax_end(pi):
                act.wait_ge(S["km_row"], pi + 1)
                act.activation(kmrow[:, 0:C], psM[0:1, 0:C], ACT.Copy, scale=-1.0).then_inc(S["km_rowc"], 1)

            def qkv_a(pi, s, q, par, i):
                m = (pi * CHUNKS + s) * QT + q
                if q == 0:
                    act.wait_ge(S[f"xp{par}"], (pi * 24 + 8 + i + 1) * 16)
                act.wait_ge(S["q_mm"], m + 1)
                affine(lambda h: gt[:, h, :], lambda h: xp[:, par, h, q * P:(q + 1) * P], "P")\
                    .then_inc(S["q_gt"], 1)
                if q == QT - 1:
                    act.wait_ge(S["q_gt"], m + 1)
                    act.sem_inc(S["xp_rel"], 1)

            def qkv_b(pi, s, q, par):
                m = (pi * CHUNKS + s) * QT + q
                act.wait_ge(S["q_mm"], m + 2)
                act.wait_ge(S["q_ctx"], m + 1)
                act.activation(ke, psP[:, 1, 0:C], ACT.Exp)
                act.activation(vv, psP[:, 1, C:2 * C], ACT.Copy).then_inc(S["q_ev"], 1)
                act.wait_ge(S["q_sub"], m + 2)
                act.activation(qe, qe, ACT.Exp).then_inc(S["q_exp"], 1)
                act.wait_ge(S["q_tr"], m + 1)
                hold(act)
                act.activation(qT[:, :, at(s * CHUNK + q * P)], psO[:, 0, 0:C].rearrange("p (h n) -> p h n", h=CH),
                               ACT.Copy).then_inc(S["q_T"], 1)

            def pre(pi, c, slot, hc):
                k = pi * CHUNKS + c
                act.wait_ge(S["nP_done"], pi * 3 + 3)
                act.wait_ge(S[f"xp{slot}"], (pi * 24 + 16 + hc + 1) * 16)
                act.wait_ge(S["l_mm"], k + 1)
                affine(lambda h: gn[:, h, :], lambda h: xp[:, slot, h, :], "P").then_inc(S["l_gn"], 1)
                act.wait_ge(S["l_gn"], k + 1)
                act.sem_inc(S["xp_rel"], 1)
                act.wait_ge(S["l_mm"], k + 2)
                hold(act)
                act.activation(x02[:, 0, at(c * CHUNK, CHUNK)], psP[:, 0, :], ACT.Identity, bias=b3[:, 0:1])
                act.activation(x02[:, 1, at(c * CHUNK, CHUNK)], psP[:, 1, :], ACT.Identity, bias=b3[:, 2:3])\
                    .then_inc(S["l_ev"], 1)

            def att(pi, s, q, par, i):
                m = (pi * CHUNKS + s) * QT + q
                act.wait_ge(S["x_own"], (pi + 1) * X_STEPS)
                for j in range(4):
                    act.wait_ge(S["a_ttr"], m * 4 + j + 1)
                    hold(act)
                    act.activation(ex[:, j % 2, :], x02[:, 0, j * 1024:(j + 1) * 1024], ACT.Exp,
                                   bias=nb[:, 2, at(s * QT + q, 1)], scale=x1c[:, at(s * QT + q, 1)],
                                   accum_out=dn[:, 0, j:j + 1]).then_inc(S["a_x"], 1)
                if q == 0:
                    act.wait_ge(S[f"xp{par}"], (pi * 24 + 20 + i + 1) * 16)
                affine(lambda h: gt[:, h, :], lambda h: xp[:, par, h, q * P:(q + 1) * P], "P")\
                    .then_inc(S["a_gt"], 1)
                act.wait_ge(S["a_tr"], m + 1)
                act.activation(xs, psP[:, 1, 0:C], ACT.Copy).then_inc(S["a_xs"], 1)
                act.wait_ge(S["a_feat"], m + 1)
                act.activation(gex[:, :], feat[:, :], ACT.Exp, scale=-1.0).then_inc(S["a_gex"], 1)

            def f_apply(c, fi, s):
                act.wait_ge(S["nF_done"], fi + 1)
                act.wait_ge(S["f_loadB"], (c + 1) * 16)
                hold(act)
                affine(lambda h: pad[:, h, at(s * ROWS + 1, ROWS), 1:W + 1],
                       lambda h: xf[:, 1, h, :].rearrange("p (r c) -> p r c", c=W), "F").then_inc(S["f_applied"], 1)

            def entries(fi, et, half, slot, odd):
                e = fi * ENTRIES + et
                act.wait_ge(S["f_applied"], (fi + 1) * CHUNKS + 1)
                act.wait_ge(S["tab_mm"], e + 1)
                hold(act)
                act.activation(stg[:, :, :], padf[:, :, at(et * P, ESPAN)], ACT.Copy).then_inc(S["staged"], 1)

            def ln_a(fi, s):
                c = fi * CHUNKS + s
                act.wait_ge(S["ln_var"], c + 1)
                act.activation(lsd[:, 1, :], lsd[:, 0, :], ACT.Sqrt).then_inc(S["ln_root"], 1)

            def ln_b(fi, s):
                c = fi * CHUNKS + s
                act.wait_ge(S["ln_scale"], c + 1)
                act.wait_ge(S["off_stored"], c + 1)
                for q in range(QT):
                    last = act.activation(ln[:, q, :], psF4[:, q, :], ACT.Identity, bias=lsd[:, 3, q:q + 1],
                                          scale=lsd[:, 2, q:q + 1])
                last.then_inc(S["ln_done"], 1)

            def ln_c(fi, s):
                c = fi * CHUNKS + s
                act.wait_ge(S["lnT"], c + 1)
                for h in range(CH):
                    last = act.activation(ge[:, h, :], psF[:, h, :], ACT.Gelu, bias=cols[:, 2, h:h + 1],
                                          scale=cols[:, 1, h:h + 1])
                last.then_inc(S["gelu"], 1)
                act.wait_ge(S["proj"], c + 2)
                act.activation(osb.rearrange("p (a n) -> p a n", a=2), psO[:, :, 0:2 * NPROJ], ACT.Copy)\
                    .then_inc(S["osb"], 1)

            def weights(n, slot, half, b, tile):
                act.wait_ge(S["lm"], n + 1)
                act.activation(lb[:, 1, :], lb[:, 0, :], ACT.Exp).then_inc(S["mexp"], 1)

            def consume(n, slot, part, half, b, tile):
                act.wait_ge(S["sampT"], n + 1)
                act.activation(sT[:, :, :], psS[:, 0, :, :], ACT.Copy).then_inc(S["sT_ready"], 1)

            schedule(act, dict(setup=setup, norm=norm, vq=vq, kmax=kmax, kmax_end=kmax_end, qkv_a=qkv_a, qkv_b=qkv_b,
                               pre=pre, att=att, f_apply=f_apply, entries=entries, ln_a=ln_a, ln_b=ln_b, ln_c=ln_c,
                               weights=weights, consume=consume))

        @block.tensor
        def _(pe):
            def mm(dst, lhsT, rhs, first=True, last=True):
                return pe.matmul(dst, lhsT, rhs, start=first, stop=last)

            def over_h(dst, lhsT, rhs, more=False):
                for h in range(CH):
                    ins = mm(dst, lhsT(h), rhs(h), h == 0, h == CH - 1 and not more)
                return ins

            def setup():
                credit(pe, "tensor")
                pe.wait_ge(S["setup_act"], 1)
                for nh in range(2):
                    ins = over_h(psP[0:1, nh, :], lambda h: const("mhalf"), lambda h: sc[:, h, nh * 512:nh * 512 + 512])
                ins.then_inc(S["setup_pe"], 1)
                pe.wait_ge(S["setup_dve"], SETUP_DVE)
                pe.wait_ge(S["setup_act"], 2)

            def norm(kind, j, st, ready, value):
                o = 508 if kind == "P" else 504
                pe.wait_ge(S[f"n{kind}_d"], j * NORM_STEPS + 2)
                mm(psM[:, o:o + 2], group_m, nrm[kind][:, 0:2, 0]).then_inc(S[f"n{kind}_p"], 1)
                pe.wait_ge(S[f"n{kind}_d"], j * NORM_STEPS + 6)
                mm(psM[:, o + 2:o + 4], group_m, nrm[kind][:, 4, :]).then_inc(S[f"n{kind}_p"], 1)

            def vq(pi, s, par, i):
                m0 = (pi * CHUNKS + s) * QT

                def scores(q):
                    m = m0 + q
                    pe.wait_ge(S["vq_sq"], m + 1)
                    pe.wait_ge(S["vq_sc"], m + 1)
                    over_h(psO[:, 1, 0:1], lambda h: sq[:, h, :], lambda h: const("mhalf"))
                    for nh in range(2):
                        k = slice(nh * 512, nh * 512 + 512)
                        over_h(psP[:, nh, :], lambda h: gt[:, h, :], lambda h: emb[:, h, k], more=True)
                        ins = mm(psP[:, nh, :], ones_m[0:1, :], e2row[:, k], False, True)
                    ins.then_inc(S["vq_mm"], 1)

                def lookup(q):
                    m = m0 + q
                    pe.wait_ge(S["vq_diag"], m + 3)
                    mm(psM[:, P:2 * P], ones_m, dg).then_inc(S["vq_bc"], 1)
                    pe.wait_ge(S["vq_hot"], m + 1)
                    for h in range(CH):
                        for k in range(CB):
                            ins = mm(psM[:, C + h * P:C + (h + 1) * P], embT[:, k, h * P:(h + 1) * P], hot[:, k, :],
                                     k == 0, k == CB - 1)
                    ins.then_inc(S["vq_q"], 1)

                pe.wait_ge(S["emb_ld"], (pi + 1) * 64)
                scores(0)
                for q in range(QT):
                    if q + 1 < QT:
                        scores(q + 1)
                    lookup(q)

            def kmax(pi, c, slot, hc):
                k = pi * CHUNKS + c
                pe.wait_ge(S["km_gn"], k + 1)
                pe.wait_ge(S["km_red"], k + 1)
                for hh in range(CH):
                    ins = over_h(psP[:, hh, :], lambda h: w_qkv[:, h, C + hh * P:C + (hh + 1) * P], lambda h: gn[:, h, :])
                ins.then_inc(S["km_mm"], 1)

            def kmax_end(pi):
                pe.wait_ge(S["km_own"], pi * 2 + 2)
                for h in range(CH):
                    ins = mm(psM[0:1, h * P:(h + 1) * P], kmx[:, h:h + 1], ident)
                ins.then_inc(S["km_row"], 1)

            def qkv_a(pi, s, q, par, i):
                m = (pi * CHUNKS + s) * QT + q
                pe.wait_ge(S["km_rowc"], pi + 1)
                pe.wait_ge(S["q_gt"], m + 1)
                pe.wait_ge(S["q_ev"], m + 1)
                pe.wait_ge(S["q_sub"], m + 1)
                over_h(psP[:, 1, :], lambda h: gt[:, h, :], lambda h: w_qkv[:, h, C:3 * C], more=True)
                mm(psP[:, 1, :], ones_m[0:1, :], kmrow[0:1, :], False, True)
                over_h(psP[:, 0, 0:C], lambda h: gt[:, h, :], lambda h: w_qkv[:, h, 0:C])\
                    .then_inc(S["q_mm"], 1)

            def qkv_b(pi, s, q, par):
                m = (pi * CHUNKS + s) * QT + q
                pe.wait_ge(S["q_ev"], m + 2)
                pe.wait_ge(S["q_acc"], m + 1)
                for h in range(CH):
                    a, k = h * (P + 1), slice(h * P, (h + 1) * P)
                    mm(psM[:, a:a + P], vv[:, k], ke[:, k])
                    ins = mm(psM[:, a + P:a + P + 1], ke[:, k], ones_m[:, 0:1])
                ins.then_inc(S["q_ctx"], 1)
                pe.wait_ge(S["q_n"], m + 1)
                pe.wait_ge(S["q_T"], m + 1)
                for h in range(CH):
                    ins = pe.transpose(psO[:, 0, h * P:(h + 1) * P], qn[:, h * P:(h + 1) * P], ident)
                ins.then_inc(S["q_tr"], 1)

            def ctx_end(pi):
                pe.wait_ge(S["m_own"], pi * 2 + 2)
                for h in range(CH):
                    ins = mm(psM[:, h * C:(h + 1) * C], cm[:, h, :], w_o2[:, h, :])
                ins.then_inc(S["m_mm"], 1)

            def outp(pi, c, slot, hc):
                k = pi * CHUNKS + c
                pe.wait_ge(S["m_done"], pi + 1)
                pe.wait_ge(S["q_T"], (pi + 1) * TILES + 1)
                pe.wait_ge(S["o_upd"], k + 1)
                for hh in range(CH):
                    ins = over_h(psP[:, hh, :], lambda h: M[:, h, hh * P:(hh + 1) * P],
                                 lambda h: qT[:, h, at(c * CHUNK, CHUNK)])
                ins.then_inc(S["o_mm"], 1)

            def pre(pi, c, slot, hc):
                k = pi * CHUNKS + c
                pe.wait_ge(S["l_gn"], k + 1)
                pe.wait_ge(S["l_ev"], k + 1)
                pe.wait_ge(S["l_red"], k + 1)
                for a in range(2):
                    over_h(psP[:, a, :], lambda h: w13[:, a, h, :], lambda h: gn[:, h, :])
                for q in range(QT):
                    ins = over_h(psM[:, q:q + 1], lambda h: gn[:, h, q * P:(q + 1) * P], lambda h: w3[:, 1, h:h + 1])
                ins.then_inc(S["l_mm"], 1)

            def att(pi, s, q, par, i):
                m = (pi * CHUNKS + s) * QT + q
                pe.wait_ge(S["a_gt"], m + 1)
                pe.wait_ge(S["a_out"], m + 1)
                for h in range(CH):
                    k = slice(h * P, (h + 1) * P)
                    pe.transpose(psP[:, 0, k], gt[:, h, :], ident)
                    ins = pe.transpose(psP[:, 1, k], xp[:, par, h, q * P:(q + 1) * P], ident)
                ins.then_inc(S["a_tr"], 1)
                if q == QT - 1:
                    pe.wait_ge(S["a_tr"], m + 1)
                    pe.sem_inc(S["xp_rel"], 1)

            def entries(fi, et, half, slot, odd):
                e = fi * ENTRIES + et
                pe.wait_ge(S["staged"], e + 1)
                pe.wait_ge(S["tab_evac"], e + 1)
                for a, o in enumerate((0, 1, PITCH, PITCH + 1)):
                    ins = over_h(psF4[:, a, :], lambda h: stg[:, h, o:o + P], lambda h: w_in[:, h, :])
                ins.then_inc(S["tab_mm"], 1)

            def ln_a(fi, s):
                c = fi * CHUNKS + s
                pe.wait_ge(S["conv_own"], (c + 1) * CONV_STEPS)
                for q in range(QT):
                    for h in range(CH):
                        ins = pe.transpose(psF4[:, q, h * P:(h + 1) * P], cv[:, h, q * P:(q + 1) * P], ident)
                ins.then_inc(S["cvT"], 1)

            def ln_b(fi, s):
                c = fi * CHUNKS + s
                pe.wait_ge(S["ln_done"], c + 1)
                for q in range(QT):
                    for h in range(CH):
                        ins = pe.transpose(psF[:, h, q * P:(q + 1) * P], ln[:, q, h * P:(h + 1) * P], ident)
                ins.then_inc(S["lnT"], 1)

            def ln_c(fi, s):
                c = fi * CHUNKS + s
                pe.wait_ge(S["gelu"], c + 1)
                for q in range(QT):
                    o = q % 2 * NPROJ
                    ins = over_h(psO[:, q // 2, o:o + NPROJ], lambda h: ge[:, h, q * P:(q + 1) * P],
                                 lambda h: w_om[:, h, :])
                ins.then_inc(S["proj"], 1)

            def consume(n, slot, part, half, b, tile):
                pe.wait_ge(S["samp_ready"], n + 3)
                pe.wait_ge(S["x1_ready"], n + 1)
                for h in range(CH):
                    ins = pe.transpose(psS[:, 0, h, :], samp[:, h * P:(h + 1) * P], ident)
                ins.then_inc(S["sampT"], 1)
                pe.wait_ge(S["sT_ready"], n + 1)
                for hh in range(CH):
                    ins = over_h(psS[:, 1, hh, :], lambda h: w_o0[:, h, hh * P:(hh + 1) * P], lambda h: sT[:, h, :])
                ins.then_inc(S["so"], 1)

            schedule(pe, dict(setup=setup, norm=norm, vq=vq, kmax=kmax, kmax_end=kmax_end, qkv_a=qkv_a, qkv_b=qkv_b,
                              ctx_end=ctx_end, out=outp, pre=pre, att=att, entries=entries, ln_a=ln_a, ln_b=ln_b,
                              ln_c=ln_c, consume=consume))

        @block.vector
        def _(dve):
            def setup():
                credit(dve, "vector")
                dve.memset(pad[:, :, :, :], 0.0).then_inc(S["setup_dve"], 1)
                dve.memset(kmrow[:, :], 0.0).then_inc(S["setup_dve"], 1)
                dve.wait_ge(S["in_parts"], LOADS)
                for a in range(2):
                    for h in range(CH):
                        dve.tensor_scalar(w13[:, a, h, :], ones_m, w3[:, 2 * a, h:h + 1], None, ALU.mult)\
                            .then_inc(S["setup_dve"], 1)
                dve.tensor_tensor(om_bc[:, 0:NOFF], om_bc[:, 0:NOFF], const("base"), ALU.add)\
                    .then_inc(S["setup_dve"], 1)
                dve.wait_ge(S["setup_dve"], SETUP_DVE)

            def norm(kind, j, st, ready, value):
                v, d, p = nrm[kind], S[f"n{kind}_d"], S[f"n{kind}_p"]
                o = 508 if kind == "P" else 504
                w = Steps(j, NORM_STEPS)
                dve.wait_ge(S[ready], value)
                hold(dve)
                for h in range(CH):
                    dve.bn_aggr(v[:, h, :], st[:, h, :, :].rearrange("p k s -> p (k s)")).then_inc(d, 1)
                    w.next()
                dve.wait_ge(p, j * 2 + 1)
                dve.tensor_copy(v[:, 2, :], psM[:, o:o + 2]).then_inc(d, 1)
                dve.wait_ge(d, w.next())
                dve.tensor_tensor(v[:, 3, :], v[:, 0:2, 0], v[:, 2, :], ALU.subtract).then_inc(d, 1)
                dve.wait_ge(d, w.next())
                dve.tensor_tensor(v[:, 7, :], v[:, 3, :], v[:, 3, :], ALU.mult).then_inc(d, 1)
                dve.wait_ge(d, w.next())
                dve.tensor_tensor(v[:, 4, :], v[:, 7, :], v[:, 0:2, 1], ALU.add).then_inc(d, 1)
                w.next()
                dve.wait_ge(p, j * 2 + 2)
                dve.tensor_scalar(v[:, 5, :], psM[:, o + 2:o + 4], EPS_GN, None, ALU.add).then_inc(d, 1)
                w.next()
                dve.wait_ge(S[f"n{kind}_a"], j + 1)
                dve.reciprocal(v[:, 8, :], v[:, 6, :]).then_inc(d, 1)
                dve.wait_ge(d, w.next())
                dve.scalar_tensor_tensor(v[:, 9, :], v[:, 2, :], -1.0, v[:, 8, :], ALU.mult, ALU.mult)\
                    .then_inc(S[f"n{kind}_done"], 1)
                w.end()

            def stats(dst, src, s, name):
                for h in range(CH):
                    dve.bn_stats(dst[:, h, at(s, 1), :].rearrange("p a b -> p (a b)"), src(h)).then_inc(S[name], 1)

            def vq(pi, s, par, i):
                for q in range(QT):
                    m = (pi * CHUNKS + s) * QT + q
                    w = Steps(m, VQ_STEPS)
                    dve.wait_ge(S["vq_sc"], m + 2)
                    hold(dve)
                    dve.max(m8[:, :], sc[:, q % 2, :]).then_inc(S["vq_own"], 1)
                    dve.wait_ge(S["vq_own"], w.next())
                    hold(dve)
                    dve.max_index(i8[:, :], m8[:, :], sc[:, q % 2, :]).then_inc(S["vq_own"], 1)
                    dve.wait_ge(S["vq_own"], w.next())
                    dve.tensor_copy(idf[:, :], i8[:, 0:1]).then_inc(S["vq_own"], 1)
                    dve.wait_ge(S["vq_own"], w.next())
                    w.end()
                    dve.tensor_scalar(dg, ident, idf[:, :], None, ALU.mult).then_inc(S["vq_diag"], 1)
                    dve.wait_ge(S["vq_bc"], m + 1)
                    dve.tensor_tensor(hot, psM[:, P:2 * P].unsqueeze(1).broadcast_to([P, CB, P]),
                                      code.unsqueeze(2).broadcast_to([P, CB, P]), ALU.is_equal)\
                        .then_inc(S["vq_hot"], 1)
                    dve.wait_ge(S["vq_q"], m + 1)
                    xq = xp[:, par, :, q * P:(q + 1) * P]
                    dve.tensor_tensor(xq, psM[:, C:2 * C].rearrange("p (h n) -> p h n", h=CH), xq, ALU.add)\
                        .then_inc(S["vq_upd"], 1)
                    if q == QT - 1:
                        dve.wait_ge(S["vq_upd"], m + 1)
                        stats(stp, lambda h: xp[:, par, h, :], s, "st_done")

            def kmax(pi, c, slot, hc):
                dve.wait_ge(S["km_mm"], pi * CHUNKS + c + 2)
                dve.tensor_reduce(km[:, :, at(c, 1)], psP[:, :, :], AX.X, ALU.max).then_inc(S["km_red"], 1)

            def kmax_end(pi):
                dve.wait_ge(S["km_red"], (pi + 1) * CHUNKS + 1)
                dve.tensor_reduce(kmx[:, :], km[:, :, :], AX.X, ALU.max).then_inc(S["km_own"], 1)
                dve.memset(ctxa[:, :, :], 0.0).then_inc(S["km_own"], 1)
                dve.wait_ge(S["km_own"], pi * 2 + 2)
                hold(dve)

            def qkv_b(pi, s, q, par):
                m = (pi * CHUNKS + s) * QT + q
                w = Steps(m, Q_STEPS)

                def heads(x):
                    return x.rearrange("p (a d) -> p a d", d=DH)

                def each(x):
                    return x.unsqueeze(2).broadcast_to([P, HEADS, DH])

                dve.wait_ge(S["q_mm"], m + 2)
                dve.tensor_reduce(qmx[:, :], heads(psP[:, 0, 0:C]), AX.X, ALU.max).then_inc(S["q_own"], 1)
                dve.wait_ge(S["q_own"], w.next())
                dve.tensor_tensor(heads(qe), heads(psP[:, 0, 0:C]), each(qmx[:, :]), ALU.subtract)\
                    .then_inc(S["q_sub"], 1)
                dve.wait_ge(S["q_exp"], m + 1)
                dve.tensor_reduce(qsm[:, :], heads(qe), AX.X, ALU.add).then_inc(S["q_own"], 1)
                dve.wait_ge(S["q_own"], w.next())
                dve.reciprocal(qmx[:, :], qsm[:, :]).then_inc(S["q_own"], 1)
                dve.wait_ge(S["q_own"], w.next())
                w.end()
                dve.scalar_tensor_tensor(heads(qn), heads(qe), DH ** -0.5, each(qmx[:, :]), ALU.mult, ALU.mult)\
                    .then_inc(S["q_n"], 1)
                dve.wait_ge(S["q_ctx"], m + 2)
                dve.tensor_tensor(ctxa[:, :, :], psM[:, 0:CH * (P + 1)].rearrange("p (h n) -> p h n", h=CH),
                                  ctxa[:, :, :], ALU.add).then_inc(S["q_acc"], 1)
                dve.wait_ge(S["q_acc"], m + 2)

            def ctx_end(pi):
                for h in range(CH):
                    dve.tensor_tensor(cm[:, h, :], ctxa[:, h, 0:P], const("heads"), ALU.mult)
                dve.reciprocal(rden[:, :], ctxa[:, :, P]).then_inc(S["m_own"], 2)
                dve.wait_ge(S["m_mm"], pi + 1)
                dve.wait_ge(S["m_own"], pi * 2 + 2)
                for h in range(CH):
                    ins = dve.tensor_scalar(M[:, h, :], psM[:, h * C:(h + 1) * C], rden[:, h:h + 1], None, ALU.mult)
                ins.then_inc(S["m_done"], 1)

            def outp(pi, c, slot, hc):
                k = pi * CHUNKS + c
                dve.wait_ge(S["o_mm"], k + 1)
                dve.wait_ge(S[f"xp{slot}"], (pi * 24 + 12 + hc + 1) * 16)
                dve.tensor_tensor(xp[:, slot, :, :], psP[:, :, :], xp[:, slot, :, :], ALU.add).then_inc(S["o_upd"], 1)
                dve.wait_ge(S["o_upd"], k + 2)
                stats(stp, lambda h: xp[:, slot, h, :], c, "st_done")

            def pre(pi, c, slot, hc):
                k = pi * CHUNKS + c
                dve.wait_ge(S["l_ev"], k + 2)
                dve.tensor_reduce(xmn[:, 0, at(c, 1)], x02[:, 0, at(c * CHUNK, CHUNK)], AX.X, ALU.max)
                dve.tensor_reduce(xmn[:, 1, at(c, 1)], x02[:, 0, at(c * CHUNK, CHUNK)], AX.X, ALU.min)
                dve.tensor_scalar(x1c[:, at(c * QT, QT)], psM[:, 0:QT], b3[:, 1:2], None, ALU.add)\
                    .then_inc(S["l_red"], 1)

            def pre_end(pi):
                w, own = Steps(pi, X_STEPS), S["x_own"]
                dve.wait_ge(S["l_red"], (pi + 1) * CHUNKS + 1)
                dve.tensor_reduce(xmm[:, 0:1], xmn[:, 0, :], AX.X, ALU.max).then_inc(own, 1)
                w.next()
                dve.tensor_reduce(xmm[:, 1:2], xmn[:, 1, :], AX.X, ALU.min).then_inc(own, 1)
                dve.wait_ge(own, w.next())
                dve.tensor_scalar(nb[:, 0, :], x1c[:, :], xmm[:, 0:1], None, ALU.mult).then_inc(own, 1)
                w.next()
                dve.tensor_scalar(nb[:, 1, :], x1c[:, :], xmm[:, 1:2], None, ALU.mult).then_inc(own, 1)
                dve.wait_ge(own, w.next())
                dve.tensor_tensor(nb[:, 0, :], nb[:, 0, :], nb[:, 1, :], ALU.max).then_inc(own, 1)
                dve.wait_ge(own, w.next())
                dve.tensor_scalar(nb[:, 2, :], nb[:, 0, :], -1.0, None, ALU.mult).then_inc(own, 1)
                w.next()
                w.end()

            def att(pi, s, q, par, i):
                m = (pi * CHUNKS + s) * QT + q
                w = Steps(m, A_STEPS)
                for j in range(4):
                    dve.wait_ge(S["a_x"], m * 4 + j + 1)
                    dve.tensor_tensor_reduce(ex[:, j % 2, :], ex[:, j % 2, :], x02[:, 1, j * 1024:(j + 1) * 1024],
                                             1.0, 0.0, ALU.mult, ALU.add, dn[:, 1, j:j + 1]).then_inc(S["a_ttr"], 1)
                dve.wait_ge(S["a_ttr"], m * 4 + 6)
                dve.tensor_reduce(dn2[:, :], dn[:, :, :], AX.X, ALU.add).then_inc(S["a_own"], 1)
                dve.wait_ge(S["a_own"], w.next())
                dve.reciprocal(rec[:, :], dn2[:, 0:1]).then_inc(S["a_own"], 1)
                dve.wait_ge(S["a_own"], w.next())
                dve.tensor_tensor(feat[:, :], dn2[:, 1:2], rec[:, :], ALU.mult).then_inc(S["a_feat"], 1)
                dve.wait_ge(S["a_gex"], m + 1)
                dve.tensor_scalar(gate1[:, :], gex[:, :], 1.0, None, ALU.add).then_inc(S["a_own"], 1)
                dve.wait_ge(S["a_own"], w.next())
                dve.reciprocal(gate[:, :], gate1[:, :]).then_inc(S["a_own"], 1)
                dve.wait_ge(S["a_own"], w.next())
                w.end()
                dve.wait_ge(S["a_xs"], m + 1)
                dve.wait_ge(S["out_free"], m + 1)
                dve.scalar_tensor_tensor(outt, psP[:, 0, 0:C], gate[:, :], xs, ALU.mult, ALU.add)\
                    .then_inc(S["a_out"], 1)

            def post_end(pi):
                dve.wait_ge(S["a_out"], (pi + 1) * TILES + 1)
                dve.sem_inc(S["big_free"], 1)

            def f_stats(c, fi, s):
                dve.wait_ge(S["f_loadA"], (c + 1) * 16)
                for h in range(CH):
                    ins = dve.bn_stats(fstat[:, h, at(s, 1), :].rearrange("p a b -> p (a b)"), xf[:, 0, h, :])
                ins.then_inc(S["f_stat"], 1)

            def entries(fi, et, half, slot, odd):
                e = fi * ENTRIES + et
                dve.wait_ge(S["tab_mm"], e + 2)
                dve.wait_ge(S["tab_free"], e + 1)
                for a in range(4):
                    ins = dve.scalar_tensor_tensor(
                        tabt[:, slot, :, a, :], bin_bc[:, :].rearrange("p (g c) -> p g c", g=G),
                        valid[:, at(et * 4 + a, 1)], psF4[:, a, :].rearrange("p (g c) -> p g c", g=G),
                        ALU.mult, ALU.add)
                ins.then_inc(S["tab_evac"], 1)

            def ln_a(fi, s):
                c = fi * CHUNKS + s
                w, own = Steps(c, CONV_STEPS), S["conv_own"]
                dve.wait_ge(S["f_applied"], (fi + 1) * CHUNKS + 1)
                dve.wait_ge(S["tab_free"], (fi + 1) * ENTRIES + 2)
                dve.wait_ge(S["proj"], c + 1)
                for k in range(K2):
                    for h in range(CH):
                        src = pad[:, h, at(s * ROWS + k // 3, ROWS), k % 3:k % 3 + W]
                        dst = cv[:, h, :].rearrange("p (r c) -> p r c", c=W)
                        if k:
                            dve.wait_ge(own, w.before + 2 * (k - 1) + h + 1)
                            dve.scalar_tensor_tensor(dst, src, dwk[:, h, k:k + 1], dst, ALU.mult, ALU.add)\
                                .then_inc(own, 1)
                        else:
                            dve.tensor_scalar(dst, src, dwk[:, h, k:k + 1], cols[:, 0, h:h + 1], ALU.mult, ALU.add)\
                                .then_inc(own, 1)
                        w.next()
                w.end()
                w, own = Steps(c, LN_STEPS), S["ln_own"]
                dve.wait_ge(S["cvT"], c + 1)
                for q in range(QT):
                    dve.bn_stats(ls6[:, q, :], psF4[:, q, :]).then_inc(own, 1)
                    w.next()
                dve.wait_ge(own, w.before + QT)
                hold(dve)
                for q in range(QT):
                    dve.bn_aggr(lmv[:, q, :], ls6[:, q, :]).then_inc(own, 1)
                    w.next()
                dve.wait_ge(own, w.before + 2 * QT)
                dve.tensor_scalar(lsd[:, 0, :], lmv[:, :, 1], EPS_LN, None, ALU.add).then_inc(S["ln_var"], 1)
                dve.wait_ge(S["ln_root"], c + 1)
                dve.reciprocal(lsd[:, 2, :], lsd[:, 1, :]).then_inc(own, 1)
                dve.wait_ge(own, w.next())
                w.end()
                dve.scalar_tensor_tensor(lsd[:, 3, :], lmv[:, :, 0], -1.0, lsd[:, 2, :], ALU.mult, ALU.mult)\
                    .then_inc(S["ln_scale"], 1)

            def weights(n, slot, half, b, tile):
                w, own = Steps(n, W_STEPS), S["w_own"]

                def points(x):
                    return x.rearrange("p (g k) -> p g k", g=G)

                def each(x):
                    return x.unsqueeze(2).broadcast_to([P, G, K2])

                dve.wait_ge(S[f"of{slot}"], (half + 1) * 16)
                dve.tensor_tensor(lb[:, 2, :], of[:, slot, NOFF:NPROJ], om_bc[:, NOFF:NPROJ], ALU.add).then_inc(own, 1)
                dve.wait_ge(own, w.next())
                dve.tensor_reduce(lg[:, 0, :], points(lb[:, 2, :]), AX.X, ALU.max).then_inc(own, 1)
                dve.wait_ge(own, w.next())
                dve.tensor_tensor(points(lb[:, 0, :]), points(lb[:, 2, :]), each(lg[:, 0, :]), ALU.subtract)\
                    .then_inc(S["lm"], 1)
                posf = pos[:, :, :].rearrange("p k a -> p (k a)")
                dve.tensor_tensor(posf, of[:, slot, 0:NOFF], om_bc[:, 0:NOFF], ALU.add).then_inc(own, 1)
                dve.wait_ge(own, w.next())
                dve.sem_inc(S["of_used"], 1)
                dve.tensor_scalar(pos[:, :, 1], pos[:, :, 1], const("trow")[:, at(tile, 1)], None, ALU.add)\
                    .then_inc(own, 1)
                dve.wait_ge(own, w.next())
                dve.tensor_scalar(posf, posf, -1.0, W + 2.0, ALU.max, ALU.min).then_inc(own, 1)
                dve.wait_ge(own, w.next())
                rndf = rnd[:, :, :].rearrange("p k a -> p (k a)")
                dve.tensor_scalar(rndf, posf, -0.5, MAGIC, ALU.add, ALU.add).then_inc(own, 1)
                dve.wait_ge(own, w.next())
                dve.tensor_scalar(rndf, rndf, -MAGIC, 0.0, ALU.add, ALU.max).then_inc(own, 1)
                dve.wait_ge(own, w.next())
                dve.tensor_scalar(rndf, rndf, float(H), None, ALU.min).then_inc(own, 1)
                dve.wait_ge(own, w.next())
                dve.scalar_tensor_tensor(ib[:, :], rnd[:, :, 1], float(PITCH), rnd[:, :, 0], ALU.mult, ALU.add)\
                    .then_inc(own, 1)
                dve.wait_ge(own, w.next())
                dve.scalar_tensor_tensor(idx[:, slot, :], ib[:, :], float(G), const("gidx"), ALU.mult, ALU.add)\
                    .then_inc(S["idx_ready"], 1)
                hatf = hat[:, :, :, :].rearrange("p a k c -> p (a k c)")
                dve.tensor_tensor(hat[:, 0, :, :], pos[:, :, :], rnd[:, :, :], ALU.subtract).then_inc(own, 1)
                dve.wait_ge(own, w.next())
                dve.tensor_scalar(hat[:, 1, :, :], hat[:, 0, :, :], -1.0, None, ALU.add).then_inc(own, 1)
                dve.wait_ge(own, w.next())
                dve.scalar_tensor_tensor(hatf, hatf, -1.0, hatf, ALU.mult, ALU.min).then_inc(own, 1)
                dve.wait_ge(own, w.next())
                dve.tensor_scalar(hatf, hatf, 1.0, 0.0, ALU.add, ALU.max).then_inc(own, 1)
                w.next()
                dve.wait_ge(S["mexp"], n + 1)
                dve.tensor_reduce(lg[:, 1, :], points(lb[:, 1, :]), AX.X, ALU.add).then_inc(own, 1)
                dve.wait_ge(own, w.next())
                dve.reciprocal(lg[:, 2, :], lg[:, 1, :]).then_inc(own, 1)
                dve.wait_ge(own, w.next())
                dve.tensor_tensor(points(lb[:, 2, :]), points(lb[:, 1, :]), each(lg[:, 2, :]), ALU.mult)\
                    .then_inc(own, 1)
                dve.wait_ge(own, w.next())
                dve.tensor_tensor(wy[:, :, :], hat[:, :, :, 1], lb[:, 2, :].unsqueeze(1).broadcast_to([P, 2, GK]),
                                  ALU.mult).then_inc(own, 1)
                dve.wait_ge(own, w.next())
                for a in range(2):
                    ins = dve.tensor_tensor(wts[:, slot, :, 2 * a:2 * a + 2],
                                            wy[:, a, :].unsqueeze(2).broadcast_to([P, GK, 2]),
                                            hat[:, :, :, 0].rearrange("p b k -> p k b"), ALU.mult)
                ins.then_inc(own, 1)
                w.next()
                w.end()

            def consume(n, slot, part, half, b, tile):
                dve.wait_ge(S["w_own"], (n + 1) * W_STEPS)
                dve.wait_ge(S[f"gath{part}{slot}"], (half + 1) * (GK * 16))
                quads = gath[:, slot, :, :].rearrange("p k (a c) -> p (k a) c", c=GC)
                dve.tensor_tensor(quads, quads,
                                  wts[:, slot, :, :].rearrange("p k a -> p (k a)").unsqueeze(2)
                                  .broadcast_to([P, GK * 4, GC]), ALU.mult).then_inc(S["c_own"], 1)
                dve.wait_ge(S["c_own"], n + 1)
                dve.tensor_reduce(samp[:, :].rearrange("p (g c) -> p g c", g=G),
                                  gath[:, slot, :, :].rearrange("p (g k) (a c) -> p g c (k a)", g=G, c=GC),
                                  AX.X, ALU.add).then_inc(S["samp_ready"], 1)
                dve.wait_ge(S["so"], n + 1)
                dve.wait_ge(S["xr_ld"], (n + 1) * 16)
                dve.wait_ge(S["x1_free"], n + 1)
                for h in range(CH):
                    ins = dve.scalar_tensor_tensor(x1t[:, h, :], psS[:, 1, h, :], cols[:, 3, h:h + 1], xr[:, h, :],
                                                   ALU.add, ALU.add)
                ins.then_inc(S["x1_ready"], 1)
                dve.wait_ge(S["x1_ready"], n + 2)
                stats(st1, lambda h: x1t[:, h, :], tile, "st1_done")

            schedule(dve, dict(setup=setup, norm=norm, vq=vq, kmax=kmax, kmax_end=kmax_end, qkv_b=qkv_b,
                               ctx_end=ctx_end, out=outp, pre=pre, pre_end=pre_end, att=att, post_end=post_end,
                               f_stats=f_stats, entries=entries, ln_a=ln_a, weights=weights, consume=consume))


SETUP_DVE = 7


def kernel(**inputs):
    import concourse.bacc as bacc
    from concourse.bass_utils import run_bass_kernel_spmd as run

    nc = bacc.Bacc("TRN2", target_bir_lowering=False, num_devices=1)
    arrays, t = {}, {}

    def put(name, a):
        a = np.ascontiguousarray(a)
        arrays[f"in_{name}"] = a
        t[name] = nc.dram_tensor(f"in_{name}", a.shape, mybir.dt.from_np(a.dtype), kind="ExternalInput").ap()

    x = np.asarray(inputs["x"])
    put("xT", x.reshape(B, N, C).transpose(0, 2, 1).reshape(B, CH, P, N))
    put("consts", constants())
    l0 = {k[8:]: np.asarray(v) for k, v in inputs.items() if k.startswith("L0_conv_")}
    for name in ("w_in", "w_off", "w_mask", "b_in", "b_off", "b_mask"):
        put(name, l0[name])
    put("w_out0", l0["w_out"])
    by_channel = [l0[k] for k in ("dw_bias", "ln_gamma", "ln_beta", "b_out")]
    by_channel += [np.asarray(inputs[f"L3_conv_w{i}"]) for i in (1, 2, 3)]
    put("cols", np.stack(by_channel).reshape(7, CH, P).transpose(2, 0, 1))
    put("dwk", l0["dw_kernel"].reshape(K2, C).T)
    put("emb", inputs["L1_conv_embeddings"])
    put("embT", np.asarray(inputs["L1_conv_embeddings"]).T)
    put("w_qkv", inputs["L2_conv_w_qkv"])
    put("w_out2", inputs["L2_conv_w_out"])
    for i in (1, 2, 3):
        put(f"b{i}", inputs[f"L3_conv_b{i}"])
    out = nc.dram_tensor("out", (B, N, C), F32, kind="ExternalOutput").ap()
    build(nc, t, out)
    r = run(nc, [arrays], core_ids=[0])
    return r.results[0]["out"].reshape(B, H, W, C)
```

```python
from contextlib import ExitStack

import numpy as np

import concourse.bass as bass
from concourse import mybir

ALU = mybir.AluOpType
ACT = mybir.ActivationFunctionType
AX = mybir.AxisListType
F32 = mybir.dt.float32
I32 = mybir.dt.int32
U32 = mybir.dt.uint32

P = 128
B, H, W, C = 8, 64, 64, 256
N = H * W
CH = C // P
G, K2 = 8, 9
GC = C // G
GK = G * K2
NOFF = 2 * GK
NPROJ = NOFF + GK
TILES = N // P
CHUNK = 512
CHUNKS = N // CHUNK
QT = CHUNK // P
ROWS = CHUNK // W
PITCH = W + 2
PROWS = H + 3
ENTRIES = 34
ESPAN = P + PITCH + 2
QUAD = 4 * GC
CODES = 1024
CB = CODES // P
HEADS, DH = 8, 32
GROUP = 8
MAGIC = 12582912.0

COLS = {}
_at = 0
for _name, _n in (("ident", P), ("group", P), ("heads", P), ("ones", P), ("valid", ENTRIES * 4),
                  ("base", NOFF),
                  ("trow", TILES), ("gidx", GK), ("code", CB), ("mhalf", 1)):
    COLS[_name] = slice(_at, _at + _n)
    _at += _n
NCONST = _at


def constants():
    c = np.zeros((P, NCONST), np.float32)
    p = np.arange(P)
    c[:, COLS["ident"]] = np.eye(P)
    c[:, COLS["group"]] = (p[:, None] // GROUP == p[None] // GROUP) / GROUP
    c[:, COLS["heads"]] = p[:, None] // DH == p[None] // DH
    c[:, COLS["ones"]] = 1
    e = np.arange(ENTRIES)[None, :, None] * P + p[:, None, None]
    q = e + np.array([0, 1, PITCH, PITCH + 1])[None, None]
    row, col = q // PITCH, q % PITCH
    c[:, COLS["valid"]] = ((row >= 1) & (row <= H) & (col >= 1) & (col <= W)).reshape(P, -1)
    ky, kx = np.meshgrid(np.arange(3) - 1, np.arange(3) - 1, indexing="ij")
    base = np.stack([1 + (p % W)[:, None] + kx.reshape(1, -1), 1 + (p // W)[:, None] + ky.reshape(1, -1)], -1)
    c[:, COLS["base"]] = np.broadcast_to(base[:, None], (P, G, K2, 2)).reshape(P, -1)
    c[:, COLS["trow"]] = np.arange(TILES)[None] * (P // W)
    c[:, COLS["gidx"]] = np.repeat(np.arange(G), K2)[None]
    c[:, COLS["code"]] = p[:, None] + np.arange(CB)[None] * P
    c[:, COLS["mhalf"]] = -0.5
    return c


class Steps:

    def __init__(self, unit, per):
        self.before, self.per, self.n = unit * per, per, 0

    def next(self):
        self.n += 1
        assert self.n <= self.per
        return self.before + self.n

    def end(self):
        assert self.n == self.per, (self.n, self.per)


W_STEPS, CONV_STEPS, LN_STEPS, NORM_STEPS, VQ_STEPS, Q_STEPS, A_STEPS, X_STEPS = 18, 2 * K2, 9, 8, 3, 3, 4, 6
HK = GK // 2
SPLIT = 6
LOADS = 16 * 15
EPS_GN, EPS_LN = 1e-5, 1e-6


def build(nc, t, out):
    ctx = ExitStack()

    def sb(name, shape, dt=F32):
        return ctx.enter_context(nc.sbuf_tensor(name, shape, dt))

    def pb(name, shape):
        return ctx.enter_context(nc.psum_tensor(name, shape, F32))

    def sem(name):
        return ctx.enter_context(nc.semaphore(name))

    def at(k, n=P):
        return bass.ds(k, n)

    with ctx:
        tables = [nc.dram_tensor(f"table{i}", (ENTRIES * P * G, QUAD), F32, kind="Internal").ap() for i in range(2)]
        offs_d = nc.dram_tensor("offsets", (B * TILES, P, NPROJ), F32, kind="Internal").ap()
        x1_d = nc.dram_tensor("x1", (B, CH, P, N), F32, kind="Internal").ap()
        x2_d = nc.dram_tensor("x2", (B, CH, P, N), F32, kind="Internal").ap()
        x3_d = nc.dram_tensor("x3", (B, CH, P, N), F32, kind="Internal").ap()
        e2_d = nc.dram_tensor("e2", (1, CODES), F32, kind="Internal").ap()

        cst = sb("cst", [P, NCONST])

        def const(name):
            return cst[:, COLS[name]]

        ident, ones_m, group_m, valid, code = (const(k) for k in ("ident", "ones", "group", "valid", "code"))
        w_in = sb("w_in", [P, CH, C])
        w_om = sb("w_om", [P, CH, NPROJ])
        w_o0 = sb("w_o0", [P, CH, C])
        wx = sb("wx", [P, 2048])
        w_qkv = wx[:, 0:CH * 3 * C].rearrange("p (h n) -> p h n", h=CH)
        ex = wx[:, :].rearrange("p (s n) -> p s n", s=2)
        w_o2 = sb("w_o2", [P, CH, C])
        dwk = sb("dwk", [P, CH, K2])
        cols = sb("cols", [P, 7, CH])
        w3 = cols[:, 4:7, :]
        w13 = sb("w13", [P, 2, CH, P])
        b3 = sb("b3", [P, 3])
        bin_bc = sb("bin_bc", [P, C])
        om_bc = sb("om_bc", [P, NPROJ])
        kmrow = sb("kmrow", [1, C])
        pad = sb("pad", [P, CH, PROWS, PITCH])
        padf = pad[:, :, :, :].rearrange("p h r c -> p h (r c)")
        fstat = sb("fstat", [P, CH, CHUNKS, 6])
        stg = sb("stg", [P, 2, CH, ESPAN])
        R2 = sb("R2", [P, 2, 1024])
        xf = R2[:, :, :].rearrange("p s (h n) -> p s h n", h=CH)
        tabt = R2[:, :, :].rearrange("p s (g a c) -> p s g a c", g=G, a=4)
        cv = R2[:, 0, :].rearrange("p (h n) -> p h n", h=CH)
        ge = cv
        ln = R2[:, 1, :].rearrange("p (q c) -> p q c", q=QT)
        osb = R2[:, 1, 0:QT * NPROJ]
        ls6 = sb("ls6", [P, QT, 6])
        lmv = sb("lmv", [P, QT, 2])
        lsd = sb("lsd", [P, 4, QT])
        gath = sb("gath", [P, 2, GK, QUAD])
        img0 = gath[:, :, :, :].rearrange("p s k q -> p (s k q)")[:, 0:CH * N].rearrange("p (h n) -> p h n", h=CH)
        idx = sb("idx", [P, 2, GK], I32)
        wts = sb("wts", [P, 2, GK, 4])
        of = sb("of", [P, 2, NPROJ])
        pos = sb("pos", [P, GK, 2])
        rnd = sb("rnd", [P, GK, 2])
        hat = sb("hat", [P, 2, GK, 2])
        wy = sb("wy", [P, 2, GK])
        lb = sb("lb", [P, 3, GK])
        lg = sb("lg", [P, 3, G])
        ib = sb("ib", [P, GK])
        samp = sb("samp", [P, C])
        sT = sb("sT", [P, CH, P])
        xr = sb("xr", [P, CH, P])
        x1t = sb("x1t", [P, CH, P])
        st1 = sb("st1", [P, CH, TILES, 6])
        xp = sb("xp", [P, 2, CH, CHUNK])
        xpf = xp[:, :, :, :].rearrange("p s h n -> p s (h n)")
        tabt0 = xpf.rearrange("p s (g a c) -> p s g a c", g=G, a=4)
        R3 = sb("R3", [P, 1280])
        gn = R3[:, 0:CH * CHUNK].rearrange("p (h n) -> p h n", h=CH)
        gt = R3[:, 0:C].rearrange("p (h n) -> p h n", h=CH)
        gts, sqs = ([R3[:, k:k + C].rearrange("p (h n) -> p h n", h=CH) for k in (o, o + 2 * C + P)]
                    for o in (0, C))
        ke, vv = R3[:, C:2 * C], R3[:, 2 * C:3 * C]
        qe, qn = R3[:, 3 * C:4 * C], R3[:, 4 * C:5 * C]
        xs, outt = R3[:, C:2 * C], R3[:, 2 * C:3 * C]
        big = sb("big", [P, 8192])
        emb = big[:, 0:2048].rearrange("p (h k) -> p h k", h=CH)
        embT = big[:, 2048:4096].rearrange("p (k c) -> p k c", k=CB)
        sc = big[:, 4096:6144].rearrange("p (s k) -> p s k", s=2)
        hot = big[:, 6144:7168].rearrange("p (k n) -> p k n", k=CB)
        qT = big[:, :].rearrange("p (h n) -> p h n", h=CH)
        x02 = qT
        e2 = big[:, 7168:8192]
        e2row = e2[0:1, :]
        m8 = sb("m8", [P, 8])
        i8 = sb("i8", [P, 8], U32)
        x2c, idf = sb("x2c", [P, 2]), sb("idf", [P, 1])
        kmx, qmx, qsm = sb("kmx", [P, CH]), sb("qmx", [P, HEADS]), sb("qsm", [P, HEADS])
        rden = sb("rden", [P, CH])
        dn, dn2 = sb("dn", [P, 2, 4]), sb("dn2", [P, 2])
        rec, feat, gex, gate = (sb(k, [P, 1]) for k in ("rec", "feat", "gex", "gate"))
        gate1 = sb("gate1", [P, 1])
        xmm = sb("xmm", [P, 2])
        dg = R3[:, 2 * C:2 * C + P]
        km = sb("km", [P, CH, CHUNKS])
        ctxa = sb("ctxa", [P, CH, P + 1])
        cm = gt
        M = sb("M", [P, CH, C])
        xmn = sb("xmn", [P, 2, CHUNKS])
        x1c = sb("x1c", [P, TILES])
        nb = sb("nb", [P, 3, TILES])
        stp = sb("stp", [P, CH, CHUNKS, 6])
        nrm = {k: sb(f"nrm{k}", [P, 10, CH]) for k in "FP"}

        psF = pb("psF", [P, 2, 512])
        psF4 = psF[:, :, :].rearrange("p b (a c) -> p (b a) c", c=C)
        psP = pb("psP", [P, 2, 512])
        psPf = psP[:, :, :].rearrange("p b n -> p (b n)")
        psP4 = psP[:, :, :].rearrange("p b (a c) -> p (b a) c", c=C)
        psFf = psF[:, :, :].rearrange("p b n -> p (b n)")

        def scores_of(q):
            return (psPf, psFf)[q % 2]

        psS = pb("psS", [P, 2, CH, P])
        psO = pb("psO", [P, 2, 512])
        psM = pb("psM", [P, 512])

        CREDITS = {
            "sync": {},
            "vector": {"f_stat": 1, "tab_evac": 2, "of_used": 2, "samp_ready": 2, "x1_ready": 1, "big_free": 1, "vq_sc": 2,
                       "vq_diag": 2, "km_red": 1, "q_sub": 1, "q_acc": 1, "o_upd": 1, "l_red": 1, "a_ttr": 2,
                       "a_out": 1, "xp_rel": 2, "tab_free": 2, "x1_free": 1, "off_stored": 1, "out_free": 1},
            "scalar": {"f_applied": 1, "q_ev": 1, "q_T": 1, "l_ev": 1},
            "tensor": {"proj": 1, "tab_mm": 3, "vq_mm": 2, "km_mm": 1, "q_mm": 1, "q_ctx": 1, "l_mm": 1},
        }
        names = """held in_parts e2st setup_dve setup_pe setup_act
            f_loadA f_loadB f_stat f_applied conv_own cvT ln_own ln_var ln_root ln_scale ln_done lnT gelu proj
            osb offst off_stored staged tab_mm tab_evac tab0 tab1 tab_free
            of0 of1 of_used lm mexp w_own idx_ready gath00 gath01 gath10 gath11 c_own samp_ready sampT sT_ready so
            x1_ready x1st xr_ld x1_free st1_done
            emb_ld big_free xp0 xp1 xp_rel xst st_done
            vq_gt vq_sq vq_mm vq_x2 vq_sc vq_own vq_diag vq_bc vq_hot vq_q vq_upd
            km_gn km_mm km_red km_own km_row km_rowc
            q_gt q_mm q_own q_sub q_ev q_exp q_n q_ctx q_acc q_tr q_T
            m_own m_mm m_done o_mm o_upd l_gn l_mm l_red l_ev x_own
            a_x a_ttr a_own a_gt a_feat a_gex a_tr a_xs a_out outst out_free
            nF_d nF_p nF_a nF_done nP_d nP_p nP_a nP_done""".split()
        S = {n: sem(n) for n in names}
        block = ctx.enter_context(nc.Block())

        def hold(eng):
            eng.sem_inc(S["held"], 1)

        def schedule(eng, w, period=1):
            ahead = "chunk_in" in w

            def do(name, *a):
                if name in w:
                    w[name](*a)

            def steps(b, first, count, beside, sampling, image_end=False, last=False, peel=False):
                def pair(i, final):
                    for par in range(2):
                        s = i * 2 + par
                        n, half = b * TILES + first + s, b * (TILES // 2) + first // 2 + i
                        part = int(first >= SPLIT * 2)
                        where = (b, first + s + 2) if not (final and image_end) else (b + 1, par)

                        def tile(k):
                            if not sampling:
                                return
                            if k == 0:
                                do("sum_a", n, par, part, first // 2 - SPLIT * part + i)
                            elif k == 1:
                                do("sum_b", n, par)
                            elif k == 2:
                                do("sum_c", n, par)
                                if not (final and image_end and last):
                                    do("weights", n + 2, par, half + 1, *where)
                            else:
                                do("tail", n, b, first + s)

                        if sampling:
                            do("tile_loads", n, b, first + s)
                            if not (final and image_end and last):
                                do("offsets_in", n + 2, par, half + 1)
                        beside(s, par, i, tile, final and par)

                turns = count // 2
                if peel or (sampling and image_end):
                    if turns == 2:
                        pair(0, False)
                    elif turns > 2:
                        with eng.Fori(0, turns - 1) as i:
                            pair(i, False)
                    pair(turns - 1, True)
                elif turns == 1:
                    pair(0, False)
                else:
                    with eng.Fori(0, turns) as i:
                        pair(i, False)

            def table(fi, et, half, slot, odd, between=lambda: None, first=False):
                do("table_a", fi, et, half, slot, odd)
                between()
                do("table_b", fi, et, half, slot, odd, first)

            def offsets(fi, c):
                for k in "abcde":
                    do("ln_" + k, fi, c)

            def image(b, sampling, post, front, odd=0, last=False):
                pi, fi = b - 1, b + 1

                def beside_vq(s, par, i, tile, final):
                    if post:
                        do("chunk_in", pi, 0, s, par, final)
                    if front:
                        do("f_stats_in", fi * CHUNKS + s, fi, s)
                    for q in range(QT):
                        if post:
                            do("vq_a", pi, s, q, par, i)
                        if front and q == 1:
                            do("f_stats", fi * CHUNKS + s, fi, s)
                        tile(q)
                        if post:
                            do("vq_b", pi, s, q, par)
                    if post:
                        do("chunk_out", pi, s, par, 0)

                def beside_kmax(s, par, i, tile, final):
                    for q in range(2):
                        if post:
                            do("chunk_in", pi, 1, s * 2 + q, q, final and q)
                        if front:
                            do("f_apply", fi * CHUNKS + s * 2 + q, fi, s * 2 + q)
                        if post:
                            do("kmax_a", pi, s * 2 + q, q, s)
                        tile(q * 2)
                        if post:
                            do("kmax_b", pi, s * 2 + q, q, s)
                        tile(q * 2 + 1)

                def beside_qkv(s, par, i, tile, final):
                    if post:
                        do("chunk_in", pi, 2, s, par, final)
                    for q in range(QT):
                        e, half, slot = s * 3 + q - 1, i * 3 + (par * 3 + q - 1) // 2, (par * 3 + q - 1) % 2
                        if post:
                            do("qkv_a", pi, s, q, par, i)
                        if front and q:
                            do("table_a", fi, e, half, slot, 1 - odd)
                        if post:
                            do("qkv_b", pi, s, q, par)
                        if front and q:
                            do("table_b", fi, e, half, slot, 1 - odd)
                        tile(q)
                        if post:
                            do("qkv_c", pi, s, q, par)

                def beside_out(s, par, i, tile, final):
                    for q in range(4):
                        if post:
                            do("chunk_in", pi, 3, s * 4 + q, q % 2, final and q == 3)
                            do("out_a", pi, s * 4 + q, q % 2, s * 2 + q // 2)
                        if front and q % 2:
                            table(fi, 24 + s * 2 + q // 2, 12 + s, q // 2, 1 - odd, lambda: tile(q))
                        else:
                            tile(q)
                        if post:
                            do("out_b", pi, s * 4 + q, q % 2, s * 2 + q // 2)
                            do("chunk_out", pi, s * 4 + q, q % 2, 1)

                def beside_pre(s, par, i, tile, final):
                    for q in range(4):
                        if post:
                            do("chunk_in", pi, 4, s * 4 + q, q % 2, final and q == 3)
                            do("pre_a", pi, s * 4 + q, q % 2, s * 2 + q // 2)
                        if front and q % 2:
                            table(fi, 28 + s * 2 + q // 2, 14 + s, q // 2, 1 - odd, lambda: tile(q))
                        else:
                            tile(q)
                        if post:
                            do("pre_b", pi, s * 4 + q, q % 2, s * 2 + q // 2)

                def beside_att(s, par, i, tile, final):
                    if post and not (last and final):
                        do("chunk_in", pi, 5, s, par, final)
                    for q in range(QT):
                        if post:
                            do("att_a", pi, s, q, par, i)
                        if front:
                            do("ln_" + "abde"[q], fi, s)
                        tile(q)
                        if post:
                            do("att_b", pi, s, q, par, i)
                        if front and q == 1:
                            do("ln_c", fi, s)

                if post:
                    do("post_start", pi)
                    do("norm", "P", pi * 3, st1, "st1_done", (pi + 1) * 2 * TILES)
                steps(b, 0, 8, beside_vq, sampling, peel=ahead)
                if post:
                    do("norm", "P", pi * 3 + 1, stp, "st_done", pi * 32 + 16)
                if front:
                    do("norm", "F", fi, fstat, "f_stat", (fi + 1) * CHUNKS + 1)
                steps(b, 8, 4, beside_kmax, sampling, peel=ahead)
                if post:
                    do("kmax_end", pi)
                steps(b, 12, 8, beside_qkv, sampling, peel=ahead)
                if post:
                    do("ctx_end", pi)
                steps(b, 20, 2, beside_out, sampling, peel=ahead)
                if post:
                    do("norm", "P", pi * 3 + 2, stp, "st_done", pi * 32 + 32)
                steps(b, 22, 2, beside_pre, sampling, peel=ahead)
                if post:
                    do("pre_end", pi)
                if front:
                    for q in range(2):
                        table(fi, ENTRIES - 2 + q, ENTRIES // 2 - 1, q, 1 - odd)
                steps(b, 24, 8, beside_att, sampling, image_end=True, last=not front, peel=ahead)
                if post:
                    do("post_end", pi)

            def first_front():
                do("first_stats")
                do("norm", "F", 0, fstat, "f_stat", CHUNKS + 1)
                do("first_apply")
                pieces = [("ln_" + k, 0, 0, True) for k in "abcde"]
                pieces += [("offsets_in", n, n, 0) for n in range(2)] + [("weights", n, n, 0, 0, n) for n in range(2)]
                pieces += [()] * (len(pieces) % 2)
                for e, piece in enumerate(pieces):
                    table(0, e, e // 2, e % 2, 0, first=True)
                    if piece:
                        do(*piece)
                with eng.Fori(len(pieces) // 2, ENTRIES // 2) as i:
                    for slot in range(2):
                        table(0, i * 2 + slot, i, slot, 0, first=True)

            def first_image():
                def all_of(tile):
                    for k in range(4):
                        tile(k)

                def beside_offsets(s, par, i, tile, final):
                    if not final:
                        offsets(0, s + 1)
                    all_of(tile)

                def beside_stats(s, par, i, tile, final):
                    for q in range(2):
                        do("f_stats_in", CHUNKS + s * 2 + q, 1, s * 2 + q)
                        do("f_stats", CHUNKS + s * 2 + q, 1, s * 2 + q)
                    all_of(tile)

                def beside_apply(s, par, i, tile, final):
                    for q in range(2):
                        do("f_apply", CHUNKS + s * 2 + q, 1, s * 2 + q)
                    all_of(tile)

                def beside_table(s, par, i, tile, final):
                    for q in range(QT):
                        table(1, s * QT + q, s * 2 + q // 2, q % 2, 1)
                    all_of(tile)

                def beside_next(s, par, i, tile, final):
                    offsets(1, s)
                    all_of(tile)

                steps(0, 0, 8, beside_offsets, True, peel=True)
                steps(0, 8, 4, beside_stats, True)
                do("norm", "F", 1, fstat, "f_stat", 2 * CHUNKS + 1)
                steps(0, 12, 4, beside_apply, True)
                steps(0, 16, 8, beside_table, True)
                for q in range(2):
                    table(1, ENTRIES - 2 + q, ENTRIES // 2 - 1, q, 1)
                steps(0, 24, 8, beside_next, True, image_end=True)
                do("first_chunk")

            do("setup")
            first_front()
            first_image()
            with eng.Fori(0, (B - 2) // period) as i:
                for k in range(period):
                    image(i * period + (1 + k), sampling=True, post=True, front=True, odd=1 - k)
            image(B - 1, sampling=True, post=True, front=False)
            image(B, sampling=False, post=True, front=False, last=True)

        def credit(eng, name):
            for k, v in CREDITS[name].items():
                eng.sem_inc(S[k], v)

        @block.sync
        def _(sp):
            def halves(dram, b, k, n):
                return dram[at(b, 1), :, :, at(k, n)].rearrange("b h p n -> p (b h) n")

            def setup():
                def ld(dst, src):
                    sp.dma_start(dst, src).then_inc(S["in_parts"], 16)

                for c in range(CHUNKS):
                    sp.dma_start(img0[:, :, c * CHUNK:(c + 1) * CHUNK], halves(t["xT"], 0, c * CHUNK, CHUNK))\
                        .then_inc(S["f_loadA"], 16)
                ld(cst[:, :], t["consts"])
                for dst, name in ((w_in, "w_in"), (w_o0, "w_out0"), (w_o2, "w_out2"), (dwk, "dwk")):
                    ld(dst[:, :, :], t[name].rearrange("(h p) n -> p h n", p=P))
                ld(w_om[:, :, 0:NOFF], t["w_off"].rearrange("(h p) n -> p h n", p=P))
                ld(w_om[:, :, NOFF:NPROJ], t["w_mask"].rearrange("(h p) n -> p h n", p=P))
                ld(cols[:, :, :], t["cols"])
                for i in range(3):
                    ld(b3[:, i:i + 1], t[f"b{i + 1}"].partition_broadcast(P))
                ld(bin_bc[:, :], t["b_in"].partition_broadcast(P))
                ld(om_bc[:, 0:NOFF], t["b_off"].partition_broadcast(P))
                ld(om_bc[:, NOFF:NPROJ], t["b_mask"].partition_broadcast(P))
                ld(emb, t["emb"].rearrange("(h p) k -> p h k", p=P))
                sp.wait_ge(S["setup_act"], 2)
                sp.dma_start(e2_d, e2row).then_inc(S["e2st"], 16)
                sp.wait_ge(S["e2st"], 16)

            def load_chunk(pi, stage, c, slot):
                src = (x1_d, x2_d, x2_d, x2_d, x3_d, x3_d)[stage]
                sp.wait_ge(S["xp_rel"], pi * 48 + stage * 8 + c + 1)
                hold(sp)
                sp.dma_start(xp[:, slot, :, :], halves(src, pi, c * CHUNK, CHUNK)).then_inc(S[f"xp{slot}"], 16)

            def first_chunk():
                load_chunk(0, 0, 0, 0)

            def chunk_in(pi, stage, c, slot, final):
                if not final:
                    load_chunk(pi, stage, c + 1, 1 - slot)
                elif stage < 5:
                    load_chunk(pi, stage + 1, 0, 0)
                else:
                    load_chunk(pi + 1, 0, 0, 0)

            def chunk_out(pi, c, slot, k):
                sp.wait_ge(S["st_done"], pi * 32 + k * 16 + (c + 1) * 2)
                hold(sp)
                sp.dma_start(halves((x2_d, x3_d)[k], pi, c * CHUNK, CHUNK), xp[:, slot, :, :]).then_inc(S["xst"], 16)
                sp.wait_ge(S["xst"], (pi * 16 + k * 8 + c + 1) * 16)
                sp.sem_inc(S["xp_rel"], 1)

            def post_start(pi):
                sp.wait_ge(S["big_free"], pi + 1)
                sp.dma_start(emb, t["emb"].rearrange("(h p) k -> p h k", p=P)).then_inc(S["emb_ld"], 16)
                sp.dma_start(e2, e2_d.rearrange("o k -> (o k)").partition_broadcast(P)).then_inc(S["emb_ld"], 16)
                sp.dma_start(embT, t["embT"].rearrange("(k p) c -> p k c", p=P)).then_inc(S["emb_ld"], 16)
                sp.dma_start(w_qkv, t["w_qkv"].rearrange("(h p) n -> p h n", p=P)).then_inc(S["emb_ld"], 16)

            def att_b(pi, s, q, par, i):
                m = (pi * CHUNKS + s) * QT + q
                sp.wait_ge(S["a_out"], m + 2)
                sp.dma_start(out[at(pi, 1), at(s * CHUNK + q * P), :].rearrange("b p c -> p (b c)"), outt)\
                    .then_inc(S["outst"], 16)
                sp.wait_ge(S["outst"], (m + 1) * 16)
                sp.sem_inc(S["out_free"], 1)

            def f_stats_in(c, fi, s):
                sp.wait_ge(S["f_stat"], c + 1)
                hold(sp)
                sp.dma_start(xf[:, 0, :, :], halves(t["xT"], fi, s * CHUNK, CHUNK)).then_inc(S["f_loadA"], 16)

            def f_apply(c, fi, s):
                sp.wait_ge(S["f_applied"], c + 1)
                hold(sp)
                sp.dma_start(xf[:, 1, :, :], halves(t["xT"], fi, s * CHUNK, CHUNK)).then_inc(S["f_loadB"], 16)

            def table_b(fi, et, half, slot, odd, first=False):
                e = fi * ENTRIES + et
                sp.wait_ge(S["tab_evac"], e * 2 + 4)
                table = tables[odd].rearrange("(e p g) q -> e p (g q)", p=P, g=G)
                sp.dma_start(table[at(et, 1), :, :].rearrange("e p q -> p (e q)"), (xpf if first else R2)[:, slot, :])\
                    .then_inc(S[f"tab{slot}"], 16)
                sp.wait_ge(S[f"tab{slot}"], (fi * (ENTRIES // 2) + half + 1) * 16)
                sp.sem_inc(S["tab_free"], 1)

            def ln_e(fi, s, first=False):
                c = fi * CHUNKS + s
                sp.wait_ge(S["osb"], c + 1)
                sp.dma_start(offs_d[at(c * QT, QT), :, :].rearrange("q p n -> p q n"),
                             osb.rearrange("p (q n) -> p q n", q=QT)).then_inc(S["offst"], 16)
                sp.wait_ge(S["offst"], (c + 1) * 16)
                sp.sem_inc(S["off_stored"], 1)

            def offsets_in(n, slot, half):
                sp.wait_ge(S["of_used"], n + 1)
                hold(sp)
                sp.dma_start(of[:, slot, :], offs_d[at(n, 1), :, :].rearrange("o p n -> p (o n)"))\
                    .then_inc(S[f"of{slot}"], 16)

            def tile_loads(n, b, tile):
                sp.wait_ge(S["x1_ready"], n + 1)
                hold(sp)
                sp.dma_start(xr[:, :, :], halves(t["xT"], b, tile * P, P)).then_inc(S["xr_ld"], 16)

            def tail(n, b, tile):
                sp.wait_ge(S["x1_ready"], n + 2)
                sp.dma_start(halves(x1_d, b, tile * P, P), x1t[:, :, :]).then_inc(S["x1st"], 16)
                sp.wait_ge(S["x1st"], (n + 1) * 16)
                sp.sem_inc(S["x1_free"], 1)

            schedule(sp, dict(setup=setup, post_start=post_start, first_chunk=first_chunk, chunk_in=chunk_in,
                              chunk_out=chunk_out, att_b=att_b, f_stats_in=f_stats_in, f_apply=f_apply,
                              table_b=table_b, ln_e=ln_e, offsets_in=offsets_in, tile_loads=tile_loads,
                              tail=tail), period=2)

        @block.gpsimd
        def _(pool):
            def pair(b, part, i, table):
                for slot in range(2):
                    n = b * TILES + (SPLIT * part + i) * 2 + slot
                    pool.wait_ge(S["idx_ready"], n + 1)
                    pool.wait_ge(S["samp_ready"], n + 1)
                    hold(pool)
                    for k in range(GK):
                        pool.indirect_dma_start(
                            gath[:, slot, k, :], None, table[:, :],
                            bass.IndirectOffsetOnAxis(ap=idx[:, slot, k:k + 1].bitcast(U32), axis=0))\
                            .then_inc(S[f"gath{part}{slot}"], 16)

            def lower(part, n):
                pool.wait_ge(S["samp_ready"], n + 2)
                hold(pool)
                pairs = (SPLIT, TILES // 2 - SPLIT)[part]
                pool.inc_swdge_sem([S[f"gath{part}{slot}"] for slot in range(2)], [pairs * GK * 16] * 2, mode="sub")

            def image(b, odd, first=False):
                for slot in range(2):
                    pool.wait_ge(S[f"tab{slot}"], (b + 1) * (ENTRIES // 2 * 16))
                hold(pool)
                for part, pairs in enumerate((SPLIT, TILES // 2 - SPLIT)):
                    pair(b, part, 0, tables[odd])
                    if part or not first:
                        lower(1 - part, b * TILES + SPLIT * 2 * part)
                    with pool.Fori(1, pairs) as i:
                        pair(b, part, i, tables[odd])

            image(0, 0, first=True)
            with pool.Fori(0, (B - 2) // 2) as i:
                for k in range(2):
                    image(i * 2 + (1 + k), 1 - k)
            image(B - 1, 1)

        @block.scalar
        def _(act):
            def setup():
                credit(act, "scalar")
                act.wait_ge(S["in_parts"], LOADS)
                act.activation(sc, emb, ACT.Square).then_inc(S["setup_act"], 1)
                act.wait_ge(S["setup_pe"], 1)
                act.activation(e2row, psPf[0:1, :], ACT.Copy).then_inc(S["setup_act"], 1)
                act.wait_ge(S["setup_dve"], SETUP_DVE)

            def affine(dst, src, kind):
                for h in range(CH):
                    last = act.activation(dst(h), src(h), ACT.Identity, bias=nrm[kind][:, 9, h:h + 1],
                                          scale=nrm[kind][:, 8, h:h + 1])
                return last

            def norm(kind, j, st, ready, value):
                act.wait_ge(S[f"n{kind}_d"], j * NORM_STEPS + 7)
                act.activation(nrm[kind][:, 6, :], nrm[kind][:, 5, :], ACT.Sqrt).then_inc(S[f"n{kind}_a"], 1)

            def vq_a(pi, s, q, par, i):
                m0 = (pi * CHUNKS + s) * QT

                def normed(q):
                    m = m0 + q
                    act.wait_ge(S["vq_mm"], m + 1)
                    affine(lambda h: gts[q % 2][:, h, :], lambda h: xp[:, par, h, q * P:(q + 1) * P], "P")\
                        .then_inc(S["vq_gt"], 1)
                    act.wait_ge(S["vq_gt"], m + 1)
                    act.activation(sqs[q % 2], gts[q % 2], ACT.Square).then_inc(S["vq_sq"], 1)

                def scored(q):
                    m = m0 + q
                    act.wait_ge(S["vq_mm"], m + 3)
                    act.wait_ge(S["vq_diag"], m + 1)
                    act.activation(x2c[:, q % 2:q % 2 + 1], psO[:, q % 2, 0:1], ACT.Copy).then_inc(S["vq_x2"], 1)

                if q == 0:
                    act.wait_ge(S["nP_done"], pi * 3 + 1)
                    act.wait_ge(S[f"xp{par}"], (pi * 24 + i + 1) * 16)
                    normed(0)
                    normed(1)
                    scored(0)
                if q + 2 < QT:
                    normed(q + 2)
                if q + 1 < QT:
                    scored(q + 1)

            def kmax_a(pi, c, slot, hc):
                k = pi * CHUNKS + c
                act.wait_ge(S["nP_done"], pi * 3 + 2)
                act.wait_ge(S[f"xp{slot}"], (pi * 24 + 4 + hc + 1) * 16)
                act.wait_ge(S["km_mm"], k + 1)
                affine(lambda h: gn[:, h, :], lambda h: xp[:, slot, h, :], "P").then_inc(S["km_gn"], 1)
                act.wait_ge(S["km_gn"], k + 1)
                act.sem_inc(S["xp_rel"], 1)

            def kmax_end(pi):
                act.wait_ge(S["km_row"], pi + 1)
                act.activation(kmrow[:, :], psM[0:1, 0:C], ACT.Copy, scale=-1.0).then_inc(S["km_rowc"], 1)

            def q_normed(pi, s, q, par):
                m = (pi * CHUNKS + s) * QT + q
                act.wait_ge(S["q_mm"], m + 1)
                affine(lambda h: gt[:, h, :], lambda h: xp[:, par, h, q * P:(q + 1) * P], "P")\
                    .then_inc(S["q_gt"], 1)
                if q == QT - 1:
                    act.wait_ge(S["q_gt"], m + 1)
                    act.sem_inc(S["xp_rel"], 1)

            def qkv_a(pi, s, q, par, i):
                if q == 0:
                    act.wait_ge(S[f"xp{par}"], (pi * 24 + 8 + i + 1) * 16)
                    q_normed(pi, s, 0, par)

            def qkv_b(pi, s, q, par):
                m = (pi * CHUNKS + s) * QT + q
                act.wait_ge(S["q_mm"], m + 2)
                act.wait_ge(S["q_ctx"], m + 1)
                act.activation(ke, psP[:, 1, 0:C], ACT.Exp)
                act.activation(vv, psP[:, 1, C:2 * C], ACT.Copy).then_inc(S["q_ev"], 1)
                act.wait_ge(S["q_sub"], m + 2)
                act.activation(qe, qe, ACT.Exp).then_inc(S["q_exp"], 1)
                if q + 1 < QT:
                    q_normed(pi, s, q + 1, par)

            def qkv_c(pi, s, q, par):
                m = (pi * CHUNKS + s) * QT + q
                act.wait_ge(S["q_tr"], m + 1)
                hold(act)
                act.activation(qT[:, :, at(s * CHUNK + q * P)], psO[:, 0, 0:C].rearrange("p (h n) -> p h n", h=CH),
                               ACT.Copy).then_inc(S["q_T"], 1)

            def pre_a(pi, c, slot, hc):
                k = pi * CHUNKS + c
                act.wait_ge(S["nP_done"], pi * 3 + 3)
                act.wait_ge(S[f"xp{slot}"], (pi * 24 + 16 + hc + 1) * 16)
                act.wait_ge(S["l_mm"], k + 1)
                affine(lambda h: gn[:, h, :], lambda h: xp[:, slot, h, :], "P").then_inc(S["l_gn"], 1)
                act.wait_ge(S["l_gn"], k + 1)
                act.sem_inc(S["xp_rel"], 1)
                act.wait_ge(S["l_mm"], k + 2)
                hold(act)
                act.activation(x02[:, 0, at(c * CHUNK, CHUNK)], psP[:, 0, :], ACT.Identity, bias=b3[:, 0:1])
                act.activation(x02[:, 1, at(c * CHUNK, CHUNK)], psP[:, 1, :], ACT.Identity, bias=b3[:, 2:3])\
                    .then_inc(S["l_ev"], 1)

            def att_a(pi, s, q, par, i):
                m = (pi * CHUNKS + s) * QT + q
                if q == 0:
                    act.wait_ge(S[f"xp{par}"], (pi * 24 + 20 + i + 1) * 16)
                affine(lambda h: gt[:, h, :], lambda h: xp[:, par, h, q * P:(q + 1) * P], "P")\
                    .then_inc(S["a_gt"], 1)
                act.wait_ge(S["x_own"], (pi + 1) * X_STEPS)
                for j in range(4):
                    act.wait_ge(S["a_ttr"], m * 4 + j + 1)
                    hold(act)
                    act.activation(ex[:, j % 2, :], x02[:, 0, j * 1024:(j + 1) * 1024], ACT.Exp,
                                   bias=nb[:, 2, at(s * QT + q, 1)], scale=x1c[:, at(s * QT + q, 1)],
                                   accum_out=dn[:, 0, j:j + 1]).then_inc(S["a_x"], 1)

            def att_b(pi, s, q, par, i):
                m = (pi * CHUNKS + s) * QT + q
                act.wait_ge(S["a_tr"], m + 1)
                act.activation(xs, psP[:, 1, 0:C], ACT.Copy).then_inc(S["a_xs"], 1)
                act.wait_ge(S["a_feat"], m + 1)
                act.activation(gex[:, :], feat[:, :], ACT.Exp, scale=-1.0).then_inc(S["a_gex"], 1)

            def first_apply():
                act.wait_ge(S["nF_done"], 1)
                act.wait_ge(S["f_loadA"], CHUNKS * 16)
                hold(act)
                with act.Fori(0, CHUNKS) as c:
                    affine(lambda h: pad[:, h, at(c * ROWS + 1, ROWS), 1:W + 1],
                           lambda h: img0[:, h, at(c * CHUNK, CHUNK)].rearrange("p (r c) -> p r c", c=W), "F")\
                        .then_inc(S["f_applied"], 1)

            def f_apply(c, fi, s):
                act.wait_ge(S["nF_done"], fi + 1)
                act.wait_ge(S["f_loadB"], (c + 1 - CHUNKS) * 16)
                hold(act)
                affine(lambda h: pad[:, h, at(s * ROWS + 1, ROWS), 1:W + 1],
                       lambda h: xf[:, 1, h, :].rearrange("p (r c) -> p r c", c=W), "F").then_inc(S["f_applied"], 1)

            def table_a(fi, et, half, slot, odd):
                e = fi * ENTRIES + et
                act.wait_ge(S["f_applied"], (fi + 1) * CHUNKS + 1)
                act.wait_ge(S["tab_mm"], e * 2 + 1)
                hold(act)
                act.activation(stg[:, slot, :, :], padf[:, :, at(et * P, ESPAN)], ACT.Copy).then_inc(S["staged"], 1)

            def ln_b(fi, s, first=False):
                c = fi * CHUNKS + s
                act.wait_ge(S["ln_var"], c + 1)
                act.activation(lsd[:, 1, :], lsd[:, 0, :], ACT.Sqrt).then_inc(S["ln_root"], 1)

            def ln_c(fi, s, first=False):
                c = fi * CHUNKS + s
                act.wait_ge(S["ln_scale"], c + 1)
                act.wait_ge(S["off_stored"], c + 1)
                for q in range(QT):
                    last = act.activation(ln[:, q, :], (psP4 if first else psF4)[:, q, :], ACT.Identity, bias=lsd[:, 3, q:q + 1],
                                          scale=lsd[:, 2, q:q + 1])
                last.then_inc(S["ln_done"], 1)

            def ln_d(fi, s, first=False):
                c = fi * CHUNKS + s
                act.wait_ge(S["lnT"], c + 1)
                for h in range(CH):
                    last = act.activation(ge[:, h, :], (psP if first else psF)[:, h, :], ACT.Gelu, bias=cols[:, 2, h:h + 1],
                                          scale=cols[:, 1, h:h + 1])
                last.then_inc(S["gelu"], 1)

            def ln_e(fi, s, first=False):
                c = fi * CHUNKS + s
                act.wait_ge(S["proj"], c + 2)
                act.activation(osb.rearrange("p (a n) -> p a n", a=2), psO[:, :, 0:2 * NPROJ], ACT.Copy)\
                    .then_inc(S["osb"], 1)

            def weights(n, slot, half, b, tile):
                act.wait_ge(S["lm"], n + 1)
                act.activation(lb[:, 1, :], lb[:, 0, :], ACT.Exp).then_inc(S["mexp"], 1)

            def sum_c(n, slot):
                act.wait_ge(S["sampT"], n + 1)
                act.activation(sT[:, :, :], psS[:, 0, :, :], ACT.Copy).then_inc(S["sT_ready"], 1)

            schedule(act, dict(setup=setup, norm=norm, vq_a=vq_a, kmax_a=kmax_a, kmax_end=kmax_end, qkv_a=qkv_a,
                               qkv_b=qkv_b, qkv_c=qkv_c, pre_a=pre_a, att_a=att_a, att_b=att_b, f_apply=f_apply,
                               first_apply=first_apply,
                               table_a=table_a, ln_b=ln_b, ln_c=ln_c, ln_d=ln_d, ln_e=ln_e, weights=weights,
                               sum_c=sum_c))

        @block.tensor
        def _(pe):
            def mm(dst, lhsT, rhs, first=True, last=True):
                return pe.matmul(dst, lhsT, rhs, start=first, stop=last)

            def over_h(dst, lhsT, rhs, more=False):
                for h in range(CH):
                    ins = mm(dst, lhsT(h), rhs(h), h == 0, h == CH - 1 and not more)
                return ins

            def setup():
                credit(pe, "tensor")
                pe.wait_ge(S["setup_act"], 1)
                for nh in range(2):
                    ins = over_h(psP[0:1, nh, :], lambda h: const("mhalf"), lambda h: sc[:, h, nh * 512:nh * 512 + 512])
                ins.then_inc(S["setup_pe"], 1)
                pe.wait_ge(S["setup_dve"], SETUP_DVE)
                pe.wait_ge(S["setup_act"], 2)

            def norm(kind, j, st, ready, value):
                o = 508 if kind == "P" else 504
                pe.wait_ge(S[f"n{kind}_d"], j * NORM_STEPS + 2)
                mm(psM[:, o:o + 2], group_m, nrm[kind][:, 0:2, 0]).then_inc(S[f"n{kind}_p"], 1)
                pe.wait_ge(S[f"n{kind}_d"], j * NORM_STEPS + 6)
                mm(psM[:, o + 2:o + 4], group_m, nrm[kind][:, 4, :]).then_inc(S[f"n{kind}_p"], 1)

            def scores(pi, s, q):
                m = (pi * CHUNKS + s) * QT + q
                pe.wait_ge(S["vq_sq"], m + 1)
                pe.wait_ge(S["vq_sc"], m + 1)
                over_h(psO[:, q % 2, 0:1], lambda h: sqs[q % 2][:, h, :], lambda h: const("mhalf"))
                for nh in range(2):
                    k = slice(nh * 512, nh * 512 + 512)
                    ins = over_h(scores_of(q)[:, k], lambda h: gts[q % 2][:, h, :], lambda h: emb[:, h, k])
                ins.then_inc(S["vq_mm"], 1)

            def spread(pi, s, q):
                m = (pi * CHUNKS + s) * QT + q
                pe.wait_ge(S["vq_diag"], m + 3)
                mm(psO[:, q % 2, P:2 * P], ones_m, dg).then_inc(S["vq_bc"], 1)

            def vq_a(pi, s, q, par, i):
                m = (pi * CHUNKS + s) * QT + q
                if q == 0:
                    pe.wait_ge(S["emb_ld"], (pi + 1) * 64)
                    scores(pi, s, 0)
                    scores(pi, s, 1)
                    spread(pi, s, 0)
                pe.wait_ge(S["vq_hot"], m + 1)
                for h in range(CH):
                    for k in range(CB):
                        ins = mm(psM[:, C + h * P:C + (h + 1) * P], embT[:, k, h * P:(h + 1) * P], hot[:, k, :],
                                 k == 0, k == CB - 1)
                ins.then_inc(S["vq_q"], 1)

            def vq_b(pi, s, q, par):
                if q + 1 < QT:
                    spread(pi, s, q + 1)
                if q + 2 < QT:
                    scores(pi, s, q + 2)

            def kmax_a(pi, c, slot, hc):
                k = pi * CHUNKS + c
                pe.wait_ge(S["km_gn"], k + 1)
                pe.wait_ge(S["km_red"], k + 1)
                for hh in range(CH):
                    ins = over_h(psP[:, hh, :], lambda h: w_qkv[:, h, C + hh * P:C + (hh + 1) * P], lambda h: gn[:, h, :])
                ins.then_inc(S["km_mm"], 1)

            def kmax_end(pi):
                pe.wait_ge(S["km_own"], pi * 2 + 2)
                for h in range(CH):
                    ins = mm(psM[0:1, h * P:(h + 1) * P], kmx[:, h:h + 1], ident)
                ins.then_inc(S["km_row"], 1)

            def project(pi, s, q):
                m = (pi * CHUNKS + s) * QT + q
                pe.wait_ge(S["km_rowc"], pi + 1)
                pe.wait_ge(S["q_gt"], m + 1)
                pe.wait_ge(S["q_ev"], m + 1)
                pe.wait_ge(S["q_sub"], m + 1)
                over_h(psP[:, 1, 0:C], lambda h: gt[:, h, :], lambda h: w_qkv[:, h, C:2 * C], more=True)
                mm(psP[:, 1, 0:C], ones_m[0:1, :], kmrow[0:1, :], False, True)
                over_h(psP[:, 1, C:2 * C], lambda h: gt[:, h, :], lambda h: w_qkv[:, h, 2 * C:3 * C])
                over_h(psP[:, 0, 0:C], lambda h: gt[:, h, :], lambda h: w_qkv[:, h, 0:C])\
                    .then_inc(S["q_mm"], 1)

            def qkv_a(pi, s, q, par, i):
                if q == 0:
                    project(pi, s, 0)

            def qkv_c(pi, s, q, par):
                m = (pi * CHUNKS + s) * QT + q
                pe.wait_ge(S["q_ev"], m + 2)
                pe.wait_ge(S["q_acc"], m + 1)
                for h in range(CH):
                    a, k = h * (P + 1), slice(h * P, (h + 1) * P)
                    mm(psM[:, a:a + P], vv[:, k], ke[:, k])
                    ins = mm(psM[:, a + P:a + P + 1], ke[:, k], ones_m[:, 0:1])
                ins.then_inc(S["q_ctx"], 1)
                if q + 1 < QT:
                    project(pi, s, q + 1)
                pe.wait_ge(S["q_n"], m + 1)
                pe.wait_ge(S["q_T"], m + 1)
                for h in range(CH):
                    ins = pe.transpose(psO[:, 0, h * P:(h + 1) * P], qn[:, h * P:(h + 1) * P], ident)
                ins.then_inc(S["q_tr"], 1)

            def ctx_end(pi):
                pe.wait_ge(S["m_own"], pi * 2 + 2)
                for h in range(CH):
                    ins = mm(psM[:, h * C:(h + 1) * C], cm[:, h, :], w_o2[:, h, :])
                ins.then_inc(S["m_mm"], 1)

            def out_a(pi, c, slot, hc):
                k = pi * CHUNKS + c
                pe.wait_ge(S["m_done"], pi + 1)
                pe.wait_ge(S["q_T"], (pi + 1) * TILES + 1)
                pe.wait_ge(S["o_upd"], k + 1)
                for hh in range(CH):
                    ins = over_h(psP[:, hh, :], lambda h: M[:, h, hh * P:(hh + 1) * P],
                                 lambda h: qT[:, h, at(c * CHUNK, CHUNK)])
                ins.then_inc(S["o_mm"], 1)

            def pre_a(pi, c, slot, hc):
                k = pi * CHUNKS + c
                pe.wait_ge(S["l_gn"], k + 1)
                pe.wait_ge(S["l_ev"], k + 1)
                pe.wait_ge(S["l_red"], k + 1)
                for a in range(2):
                    over_h(psP[:, a, :], lambda h: w13[:, a, h, :], lambda h: gn[:, h, :])
                for q in range(QT):
                    ins = over_h(psM[:, q:q + 1], lambda h: gn[:, h, q * P:(q + 1) * P], lambda h: w3[:, 1, h:h + 1])
                ins.then_inc(S["l_mm"], 1)

            def att_a(pi, s, q, par, i):
                m = (pi * CHUNKS + s) * QT + q
                pe.wait_ge(S["a_gt"], m + 1)
                pe.wait_ge(S["a_out"], m + 1)
                for h in range(CH):
                    k = slice(h * P, (h + 1) * P)
                    pe.transpose(psP[:, 0, k], gt[:, h, :], ident)
                    ins = pe.transpose(psP[:, 1, k], xp[:, par, h, q * P:(q + 1) * P], ident)
                ins.then_inc(S["a_tr"], 1)
                if q == QT - 1:
                    pe.wait_ge(S["a_tr"], m + 1)
                    pe.sem_inc(S["xp_rel"], 1)

            def table_a(fi, et, half, slot, odd):
                e = fi * ENTRIES + et
                pe.wait_ge(S["staged"], e + 1)
                for a, o in enumerate((0, 1, PITCH, PITCH + 1)):
                    if a % 2 == 0:
                        pe.wait_ge(S["tab_evac"], e * 2 + a // 2 + 1)
                    ins = over_h(psF4[:, a, :], lambda h: stg[:, slot, h, o:o + P], lambda h: w_in[:, h, :])
                    if a % 2:
                        ins.then_inc(S["tab_mm"], 1)

            def ln_a(fi, s, first=False):
                c = fi * CHUNKS + s
                pe.wait_ge(S["conv_own"], (c + 1) * CONV_STEPS)
                for q in range(QT):
                    for h in range(CH):
                        ins = pe.transpose((psP4 if first else psF4)[:, q, h * P:(h + 1) * P], cv[:, h, q * P:(q + 1) * P], ident)
                ins.then_inc(S["cvT"], 1)

            def ln_c(fi, s, first=False):
                c = fi * CHUNKS + s
                pe.wait_ge(S["ln_done"], c + 1)
                for q in range(QT):
                    for h in range(CH):
                        ins = pe.transpose((psP if first else psF)[:, h, q * P:(q + 1) * P],
                                           ln[:, q, h * P:(h + 1) * P], ident)
                ins.then_inc(S["lnT"], 1)

            def ln_d(fi, s, first=False):
                c = fi * CHUNKS + s
                pe.wait_ge(S["gelu"], c + 1)
                for q in range(QT):
                    o = q % 2 * NPROJ
                    ins = over_h(psO[:, q // 2, o:o + NPROJ], lambda h: ge[:, h, q * P:(q + 1) * P],
                                 lambda h: w_om[:, h, :])
                ins.then_inc(S["proj"], 1)

            def sum_c(n, slot):
                pe.wait_ge(S["samp_ready"], n + 3)
                pe.wait_ge(S["x1_ready"], n + 1)
                for h in range(CH):
                    ins = pe.transpose(psS[:, 0, h, :], samp[:, h * P:(h + 1) * P], ident)
                ins.then_inc(S["sampT"], 1)

            def tail(n, b, tile):
                pe.wait_ge(S["sT_ready"], n + 1)
                for hh in range(CH):
                    ins = over_h(psS[:, 1, hh, :], lambda h: w_o0[:, h, hh * P:(hh + 1) * P], lambda h: sT[:, h, :])
                ins.then_inc(S["so"], 1)

            schedule(pe, dict(setup=setup, norm=norm, vq_a=vq_a, vq_b=vq_b, kmax_a=kmax_a, kmax_end=kmax_end, qkv_a=qkv_a,
                              qkv_c=qkv_c, ctx_end=ctx_end, out_a=out_a, pre_a=pre_a, att_a=att_a,
                              table_a=table_a, ln_a=ln_a, ln_c=ln_c, ln_d=ln_d, sum_c=sum_c, tail=tail))

        @block.vector
        def _(dve):
            def setup():
                credit(dve, "vector")
                dve.memset(pad[:, :, :, :], 0.0).then_inc(S["setup_dve"], 1)
                dve.wait_ge(S["in_parts"], LOADS)
                for a in range(2):
                    for h in range(CH):
                        dve.tensor_scalar(w13[:, a, h, :], ones_m, w3[:, 2 * a, h:h + 1], None, ALU.mult)\
                            .then_inc(S["setup_dve"], 1)
                dve.tensor_tensor(om_bc[:, 0:NOFF], om_bc[:, 0:NOFF], const("base"), ALU.add)\
                    .then_inc(S["setup_dve"], 1)
                dve.wait_ge(S["setup_dve"], SETUP_DVE)

            def norm(kind, j, st, ready, value):
                v, d, p = nrm[kind], S[f"n{kind}_d"], S[f"n{kind}_p"]
                o = 508 if kind == "P" else 504
                w = Steps(j, NORM_STEPS)
                dve.wait_ge(S[ready], value)
                hold(dve)
                for h in range(CH):
                    dve.bn_aggr(v[:, h, :], st[:, h, :, :].rearrange("p k s -> p (k s)")).then_inc(d, 1)
                    w.next()
                dve.wait_ge(p, j * 2 + 1)
                dve.tensor_copy(v[:, 2, :], psM[:, o:o + 2]).then_inc(d, 1)
                dve.wait_ge(d, w.next())
                dve.tensor_tensor(v[:, 3, :], v[:, 0:2, 0], v[:, 2, :], ALU.subtract).then_inc(d, 1)
                dve.wait_ge(d, w.next())
                dve.tensor_tensor(v[:, 7, :], v[:, 3, :], v[:, 3, :], ALU.mult).then_inc(d, 1)
                dve.wait_ge(d, w.next())
                dve.tensor_tensor(v[:, 4, :], v[:, 7, :], v[:, 0:2, 1], ALU.add).then_inc(d, 1)
                w.next()
                dve.wait_ge(p, j * 2 + 2)
                dve.tensor_scalar(v[:, 5, :], psM[:, o + 2:o + 4], EPS_GN, None, ALU.add).then_inc(d, 1)
                w.next()
                dve.wait_ge(S[f"n{kind}_a"], j + 1)
                dve.reciprocal(v[:, 8, :], v[:, 6, :]).then_inc(d, 1)
                dve.wait_ge(d, w.next())
                dve.scalar_tensor_tensor(v[:, 9, :], v[:, 2, :], -1.0, v[:, 8, :], ALU.mult, ALU.mult)\
                    .then_inc(S[f"n{kind}_done"], 1)
                w.end()

            def stats(dst, src, s, name):
                for h in range(CH):
                    dve.bn_stats(dst[:, h, at(s, 1), :].rearrange("p a b -> p (a b)"), src(h)).then_inc(S[name], 1)

            def nearest(pi, s, q):
                m = (pi * CHUNKS + s) * QT + q
                w = Steps(m, VQ_STEPS)
                dve.wait_ge(S["emb_ld"], (pi + 1) * 64)
                dve.wait_ge(S["vq_x2"], m + 1)
                dve.scalar_tensor_tensor(sc[:, q % 2, :], scores_of(q), x2c[:, q % 2:q % 2 + 1], e2, ALU.add, ALU.add)\
                    .then_inc(S["vq_sc"], 1)
                dve.wait_ge(S["vq_sc"], m + 3)
                hold(dve)
                dve.max(m8[:, :], sc[:, q % 2, :]).then_inc(S["vq_own"], 1)
                dve.wait_ge(S["vq_own"], w.next())
                hold(dve)
                dve.max_index(i8[:, :], m8[:, :], sc[:, q % 2, :]).then_inc(S["vq_own"], 1)
                dve.wait_ge(S["vq_own"], w.next())
                dve.tensor_copy(idf[:, :], i8[:, 0:1]).then_inc(S["vq_own"], 1)
                dve.wait_ge(S["vq_own"], w.next())
                w.end()
                dve.tensor_scalar(dg, ident, idf[:, :], None, ALU.mult).then_inc(S["vq_diag"], 1)

            def vq_a(pi, s, q, par, i):
                m = (pi * CHUNKS + s) * QT + q
                if q == 0:
                    nearest(pi, s, 0)
                dve.wait_ge(S["vq_bc"], m + 1)
                dve.tensor_tensor(hot, psO[:, q % 2, P:2 * P].unsqueeze(1).broadcast_to([P, CB, P]),
                                  code.unsqueeze(2).broadcast_to([P, CB, P]), ALU.is_equal)\
                    .then_inc(S["vq_hot"], 1)

            def vq_b(pi, s, q, par):
                m = (pi * CHUNKS + s) * QT + q
                if q + 1 < QT:
                    nearest(pi, s, q + 1)
                dve.wait_ge(S["vq_q"], m + 1)
                xq = xp[:, par, :, q * P:(q + 1) * P]
                dve.tensor_tensor(xq, psM[:, C:2 * C].rearrange("p (h n) -> p h n", h=CH), xq, ALU.add)\
                    .then_inc(S["vq_upd"], 1)
                if q == QT - 1:
                    dve.wait_ge(S["vq_upd"], m + 1)
                    stats(stp, lambda h: xp[:, par, h, :], s, "st_done")

            def kmax_b(pi, c, slot, hc):
                dve.wait_ge(S["km_mm"], pi * CHUNKS + c + 2)
                dve.tensor_reduce(km[:, :, at(c, 1)], psP[:, :, :], AX.X, ALU.max).then_inc(S["km_red"], 1)

            def kmax_end(pi):
                dve.wait_ge(S["km_red"], (pi + 1) * CHUNKS + 1)
                dve.tensor_reduce(kmx[:, :], km[:, :, :], AX.X, ALU.max).then_inc(S["km_own"], 1)
                dve.memset(ctxa[:, :, :], 0.0).then_inc(S["km_own"], 1)
                dve.wait_ge(S["km_own"], pi * 2 + 2)
                hold(dve)

            def heads(x):
                return x.rearrange("p (a d) -> p a d", d=DH)

            def each_head(x):
                return x.unsqueeze(2).broadcast_to([P, HEADS, DH])

            def qkv_b(pi, s, q, par):
                m = (pi * CHUNKS + s) * QT + q
                w = Steps(m, Q_STEPS)
                dve.wait_ge(S["q_mm"], m + 2)
                dve.tensor_reduce(qmx[:, :], heads(psP[:, 0, 0:C]), AX.X, ALU.max).then_inc(S["q_own"], 1)
                dve.wait_ge(S["q_own"], w.next())
                dve.tensor_tensor(heads(qe), heads(psP[:, 0, 0:C]), each_head(qmx[:, :]), ALU.subtract)\
                    .then_inc(S["q_sub"], 1)

            def qkv_c(pi, s, q, par):
                m = (pi * CHUNKS + s) * QT + q
                w = Steps(m, Q_STEPS)
                w.next()
                dve.wait_ge(S["q_exp"], m + 1)
                dve.tensor_reduce(qsm[:, :], heads(qe), AX.X, ALU.add).then_inc(S["q_own"], 1)
                dve.wait_ge(S["q_own"], w.next())
                dve.reciprocal(qmx[:, :], qsm[:, :]).then_inc(S["q_own"], 1)
                dve.wait_ge(S["q_own"], w.next())
                w.end()
                dve.scalar_tensor_tensor(heads(qn), heads(qe), DH ** -0.5, each_head(qmx[:, :]), ALU.mult, ALU.mult)\
                    .then_inc(S["q_n"], 1)
                dve.wait_ge(S["q_ctx"], m + 2)
                dve.tensor_tensor(ctxa[:, :, :], psM[:, 0:CH * (P + 1)].rearrange("p (h n) -> p h n", h=CH),
                                  ctxa[:, :, :], ALU.add).then_inc(S["q_acc"], 1)
                dve.wait_ge(S["q_acc"], m + 2)

            def ctx_end(pi):
                for h in range(CH):
                    dve.tensor_tensor(cm[:, h, :], ctxa[:, h, 0:P], const("heads"), ALU.mult)
                dve.reciprocal(rden[:, :], ctxa[:, :, P]).then_inc(S["m_own"], 2)
                dve.wait_ge(S["m_mm"], pi + 1)
                dve.wait_ge(S["m_own"], pi * 2 + 2)
                for h in range(CH):
                    ins = dve.tensor_scalar(M[:, h, :], psM[:, h * C:(h + 1) * C], rden[:, h:h + 1], None, ALU.mult)
                ins.then_inc(S["m_done"], 1)

            def out_b(pi, c, slot, hc):
                k = pi * CHUNKS + c
                dve.wait_ge(S["o_mm"], k + 1)
                dve.wait_ge(S[f"xp{slot}"], (pi * 24 + 12 + hc + 1) * 16)
                dve.tensor_tensor(xp[:, slot, :, :], psP[:, :, :], xp[:, slot, :, :], ALU.add).then_inc(S["o_upd"], 1)
                dve.wait_ge(S["o_upd"], k + 2)
                stats(stp, lambda h: xp[:, slot, h, :], c, "st_done")

            def pre_b(pi, c, slot, hc):
                k = pi * CHUNKS + c
                dve.wait_ge(S["l_ev"], k + 2)
                dve.tensor_reduce(xmn[:, 0, at(c, 1)], x02[:, 0, at(c * CHUNK, CHUNK)], AX.X, ALU.max)
                dve.tensor_reduce(xmn[:, 1, at(c, 1)], x02[:, 0, at(c * CHUNK, CHUNK)], AX.X, ALU.min)
                dve.tensor_scalar(x1c[:, at(c * QT, QT)], psM[:, 0:QT], b3[:, 1:2], None, ALU.add)\
                    .then_inc(S["l_red"], 1)

            def pre_end(pi):
                w, own = Steps(pi, X_STEPS), S["x_own"]
                dve.wait_ge(S["l_red"], (pi + 1) * CHUNKS + 1)
                dve.tensor_reduce(xmm[:, 0:1], xmn[:, 0, :], AX.X, ALU.max).then_inc(own, 1)
                w.next()
                dve.tensor_reduce(xmm[:, 1:2], xmn[:, 1, :], AX.X, ALU.min).then_inc(own, 1)
                dve.wait_ge(own, w.next())
                dve.tensor_scalar(nb[:, 0, :], x1c[:, :], xmm[:, 0:1], None, ALU.mult).then_inc(own, 1)
                w.next()
                dve.tensor_scalar(nb[:, 1, :], x1c[:, :], xmm[:, 1:2], None, ALU.mult).then_inc(own, 1)
                dve.wait_ge(own, w.next())
                dve.tensor_tensor(nb[:, 0, :], nb[:, 0, :], nb[:, 1, :], ALU.max).then_inc(own, 1)
                dve.wait_ge(own, w.next())
                dve.tensor_scalar(nb[:, 2, :], nb[:, 0, :], -1.0, None, ALU.mult).then_inc(own, 1)
                w.next()
                w.end()

            def att_a(pi, s, q, par, i):
                m = (pi * CHUNKS + s) * QT + q
                w = Steps(m, A_STEPS)
                for j in range(4):
                    dve.wait_ge(S["a_x"], m * 4 + j + 1)
                    dve.tensor_tensor_reduce(ex[:, j % 2, :], ex[:, j % 2, :], x02[:, 1, j * 1024:(j + 1) * 1024],
                                             1.0, 0.0, ALU.mult, ALU.add, dn[:, 1, j:j + 1]).then_inc(S["a_ttr"], 1)
                dve.wait_ge(S["a_ttr"], m * 4 + 6)
                dve.tensor_reduce(dn2[:, :], dn[:, :, :], AX.X, ALU.add).then_inc(S["a_own"], 1)
                dve.wait_ge(S["a_own"], w.next())
                dve.reciprocal(rec[:, :], dn2[:, 0:1]).then_inc(S["a_own"], 1)
                dve.wait_ge(S["a_own"], w.next())
                dve.tensor_tensor(feat[:, :], dn2[:, 1:2], rec[:, :], ALU.mult).then_inc(S["a_feat"], 1)

            def att_b(pi, s, q, par, i):
                m = (pi * CHUNKS + s) * QT + q
                w = Steps(m, A_STEPS)
                for k in range(2):
                    w.next()
                dve.wait_ge(S["a_gex"], m + 1)
                dve.tensor_scalar(gate1[:, :], gex[:, :], 1.0, None, ALU.add).then_inc(S["a_own"], 1)
                dve.wait_ge(S["a_own"], w.next())
                dve.reciprocal(gate[:, :], gate1[:, :]).then_inc(S["a_own"], 1)
                dve.wait_ge(S["a_own"], w.next())
                w.end()
                dve.wait_ge(S["a_xs"], m + 1)
                dve.wait_ge(S["out_free"], m + 1)
                dve.scalar_tensor_tensor(outt, psP[:, 0, 0:C], gate[:, :], xs, ALU.mult, ALU.add)\
                    .then_inc(S["a_out"], 1)

            def post_end(pi):
                dve.wait_ge(S["out_free"], (pi + 1) * TILES + 1)
                dve.sem_inc(S["big_free"], 1)

            def first_stats():
                dve.wait_ge(S["f_loadA"], CHUNKS * 16)
                hold(dve)
                with dve.Fori(0, CHUNKS) as c:
                    for h in range(CH):
                        ins = dve.bn_stats(fstat[:, h, at(c, 1), :].rearrange("p a b -> p (a b)"),
                                           img0[:, h, at(c * CHUNK, CHUNK)])
                    ins.then_inc(S["f_stat"], 1)

            def f_stats(c, fi, s):
                dve.wait_ge(S["f_loadA"], (c + 1) * 16)
                for h in range(CH):
                    ins = dve.bn_stats(fstat[:, h, at(s, 1), :].rearrange("p a b -> p (a b)"), xf[:, 0, h, :])
                ins.then_inc(S["f_stat"], 1)

            def table_b(fi, et, half, slot, odd, first=False):
                e = fi * ENTRIES + et
                dve.wait_ge(S["tab_free"], e + 1)
                for a in range(4):
                    if a % 2 == 0:
                        dve.wait_ge(S["tab_mm"], e * 2 + a // 2 + 4)
                    ins = dve.scalar_tensor_tensor(
                        (tabt0 if first else tabt)[:, slot, :, a, :], bin_bc[:, :].rearrange("p (g c) -> p g c", g=G),
                        valid[:, at(et * 4 + a, 1)], psF4[:, a, :].rearrange("p (g c) -> p g c", g=G),
                        ALU.mult, ALU.add)
                    if a % 2:
                        ins.then_inc(S["tab_evac"], 1)

            def ln_a(fi, s, first=False):
                c = fi * CHUNKS + s
                w, own = Steps(c, CONV_STEPS), S["conv_own"]
                dve.wait_ge(S["f_applied"], (fi + 1) * CHUNKS + 1)
                if not first:
                    dve.wait_ge(S["tab_free"], (fi + 1) * ENTRIES + 2)
                dve.wait_ge(S["proj"], c + 1)
                for k in range(K2):
                    for h in range(CH):
                        src = pad[:, h, at(s * ROWS + k // 3, ROWS), k % 3:k % 3 + W]
                        dst = cv[:, h, :].rearrange("p (r c) -> p r c", c=W)
                        if k:
                            dve.wait_ge(own, w.before + 2 * (k - 1) + h + 1)
                            dve.scalar_tensor_tensor(dst, src, dwk[:, h, k:k + 1], dst, ALU.mult, ALU.add)\
                                .then_inc(own, 1)
                        else:
                            dve.tensor_scalar(dst, src, dwk[:, h, k:k + 1], cols[:, 0, h:h + 1], ALU.mult, ALU.add)\
                                .then_inc(own, 1)
                        w.next()
                w.end()

            def ln_b(fi, s, first=False):
                c = fi * CHUNKS + s
                w, own = Steps(c, LN_STEPS), S["ln_own"]
                dve.wait_ge(S["cvT"], c + 1)
                for q in range(QT):
                    dve.bn_stats(ls6[:, q, :], (psP4 if first else psF4)[:, q, :]).then_inc(own, 1)
                    w.next()
                dve.wait_ge(own, w.before + QT)
                hold(dve)
                for q in range(QT):
                    dve.bn_aggr(lmv[:, q, :], ls6[:, q, :]).then_inc(own, 1)
                    w.next()
                dve.wait_ge(own, w.before + 2 * QT)
                dve.tensor_scalar(lsd[:, 0, :], lmv[:, :, 1], EPS_LN, None, ALU.add).then_inc(S["ln_var"], 1)

            def ln_c(fi, s, first=False):
                c = fi * CHUNKS + s
                own = S["ln_own"]
                dve.wait_ge(S["ln_root"], c + 1)
                dve.reciprocal(lsd[:, 2, :], lsd[:, 1, :]).then_inc(own, 1)
                dve.wait_ge(own, (c + 1) * LN_STEPS)
                dve.scalar_tensor_tensor(lsd[:, 3, :], lmv[:, :, 0], -1.0, lsd[:, 2, :], ALU.mult, ALU.mult)\
                    .then_inc(S["ln_scale"], 1)

            def weights(n, slot, half, b, tile):
                w, own = Steps(n, W_STEPS), S["w_own"]

                def points(x):
                    return x.rearrange("p (g k) -> p g k", g=G)

                def each(x):
                    return x.unsqueeze(2).broadcast_to([P, G, K2])

                dve.wait_ge(S[f"of{slot}"], (half + 1) * 16)
                dve.tensor_tensor(lb[:, 2, :], of[:, slot, NOFF:NPROJ], om_bc[:, NOFF:NPROJ], ALU.add).then_inc(own, 1)
                dve.wait_ge(own, w.next())
                dve.tensor_reduce(lg[:, 0, :], points(lb[:, 2, :]), AX.X, ALU.max).then_inc(own, 1)
                dve.wait_ge(own, w.next())
                dve.tensor_tensor(points(lb[:, 0, :]), points(lb[:, 2, :]), each(lg[:, 0, :]), ALU.subtract)\
                    .then_inc(S["lm"], 1)
                posf = pos[:, :, :].rearrange("p k a -> p (k a)")
                dve.tensor_tensor(posf, of[:, slot, 0:NOFF], om_bc[:, 0:NOFF], ALU.add).then_inc(own, 1)
                dve.wait_ge(own, w.next())
                dve.sem_inc(S["of_used"], 1)
                dve.tensor_scalar(pos[:, :, 1], pos[:, :, 1], const("trow")[:, at(tile, 1)], None, ALU.add)\
                    .then_inc(own, 1)
                dve.wait_ge(own, w.next())
                dve.tensor_scalar(posf, posf, -1.0, W + 2.0, ALU.max, ALU.min).then_inc(own, 1)
                dve.wait_ge(own, w.next())
                rndf = rnd[:, :, :].rearrange("p k a -> p (k a)")
                dve.tensor_scalar(rndf, posf, -0.5, MAGIC, ALU.add, ALU.add).then_inc(own, 1)
                dve.wait_ge(own, w.next())
                dve.tensor_scalar(rndf, rndf, -MAGIC, 0.0, ALU.add, ALU.max).then_inc(own, 1)
                dve.wait_ge(own, w.next())
                dve.tensor_scalar(rndf, rndf, float(H), None, ALU.min).then_inc(own, 1)
                dve.wait_ge(own, w.next())
                dve.scalar_tensor_tensor(ib[:, :], rnd[:, :, 1], float(PITCH), rnd[:, :, 0], ALU.mult, ALU.add)\
                    .then_inc(own, 1)
                dve.wait_ge(own, w.next())
                dve.scalar_tensor_tensor(idx[:, slot, :], ib[:, :], float(G), const("gidx"), ALU.mult, ALU.add)\
                    .then_inc(S["idx_ready"], 1)
                hatf = hat[:, :, :, :].rearrange("p a k c -> p (a k c)")
                dve.tensor_tensor(hat[:, 0, :, :], pos[:, :, :], rnd[:, :, :], ALU.subtract).then_inc(own, 1)
                dve.wait_ge(own, w.next())
                dve.tensor_scalar(hat[:, 1, :, :], hat[:, 0, :, :], -1.0, None, ALU.add).then_inc(own, 1)
                dve.wait_ge(own, w.next())
                dve.scalar_tensor_tensor(hatf, hatf, -1.0, hatf, ALU.mult, ALU.min).then_inc(own, 1)
                dve.wait_ge(own, w.next())
                dve.tensor_scalar(hatf, hatf, 1.0, 0.0, ALU.add, ALU.max).then_inc(own, 1)
                w.next()
                dve.wait_ge(S["mexp"], n + 1)
                dve.tensor_reduce(lg[:, 1, :], points(lb[:, 1, :]), AX.X, ALU.add).then_inc(own, 1)
                dve.wait_ge(own, w.next())
                dve.reciprocal(lg[:, 2, :], lg[:, 1, :]).then_inc(own, 1)
                dve.wait_ge(own, w.next())
                dve.tensor_tensor(points(lb[:, 2, :]), points(lb[:, 1, :]), each(lg[:, 2, :]), ALU.mult)\
                    .then_inc(own, 1)
                dve.wait_ge(own, w.next())
                dve.tensor_tensor(wy[:, :, :], hat[:, :, :, 1], lb[:, 2, :].unsqueeze(1).broadcast_to([P, 2, GK]),
                                  ALU.mult).then_inc(own, 1)
                dve.wait_ge(own, w.next())
                for a in range(2):
                    ins = dve.tensor_tensor(wts[:, slot, :, 2 * a:2 * a + 2],
                                            wy[:, a, :].unsqueeze(2).broadcast_to([P, GK, 2]),
                                            hat[:, :, :, 0].rearrange("p b k -> p k b"), ALU.mult)
                ins.then_inc(own, 1)
                w.next()
                w.end()

            def products(n, slot, j):
                k = slice(j * HK, (j + 1) * HK)
                quads = gath[:, slot, k, :].rearrange("p k (a c) -> p (k a) c", c=GC)
                dve.tensor_tensor(quads, quads,
                                  wts[:, slot, k, :].rearrange("p k a -> p (k a)").unsqueeze(2)
                                  .broadcast_to([P, HK * 4, GC]), ALU.mult).then_inc(S["c_own"], 1)

            def added(n, slot, j):
                dve.wait_ge(S["c_own"], n * 2 + j + 1)
                return dve.tensor_reduce(
                    samp[:, j * P:(j + 1) * P].rearrange("p (g c) -> p g c", g=G // 2),
                    gath[:, slot, j * HK:(j + 1) * HK, :].rearrange("p (g k) (a c) -> p g c (k a)", g=G // 2, c=GC),
                    AX.X, ALU.add)

            def sum_a(n, slot, part, half):
                dve.wait_ge(S["w_own"], (n + 1) * W_STEPS)
                dve.wait_ge(S[f"gath{part}{slot}"], (half + 1) * (GK * 16))
                products(n, slot, 0)

            def sum_b(n, slot):
                added(n, slot, 0)
                products(n, slot, 1)

            def sum_c(n, slot):
                added(n, slot, 1).then_inc(S["samp_ready"], 1)

            def tail(n, b, tile):
                dve.wait_ge(S["so"], n + 1)
                dve.wait_ge(S["xr_ld"], (n + 1) * 16)
                dve.wait_ge(S["x1_free"], n + 1)
                for h in range(CH):
                    ins = dve.scalar_tensor_tensor(x1t[:, h, :], psS[:, 1, h, :], cols[:, 3, h:h + 1], xr[:, h, :],
                                                   ALU.add, ALU.add)
                ins.then_inc(S["x1_ready"], 1)
                dve.wait_ge(S["x1_ready"], n + 2)
                stats(st1, lambda h: x1t[:, h, :], tile, "st1_done")

            schedule(dve, dict(setup=setup, norm=norm, vq_a=vq_a, vq_b=vq_b, kmax_b=kmax_b, kmax_end=kmax_end,
                               qkv_b=qkv_b, qkv_c=qkv_c, ctx_end=ctx_end, out_b=out_b, pre_b=pre_b, pre_end=pre_end,
                               att_a=att_a, att_b=att_b, post_end=post_end, first_stats=first_stats, f_stats=f_stats, table_b=table_b,
                               ln_a=ln_a, ln_b=ln_b, ln_c=ln_c, weights=weights, sum_a=sum_a, sum_b=sum_b,
                               sum_c=sum_c, tail=tail))


SETUP_DVE = 6


def kernel(**inputs):
    import concourse.bacc as bacc
    from concourse.bass_utils import run_bass_kernel_spmd as run

    nc = bacc.Bacc("TRN2", target_bir_lowering=False, num_devices=1)
    arrays, t = {}, {}

    def put(name, a):
        a = np.ascontiguousarray(a)
        arrays[f"in_{name}"] = a
        t[name] = nc.dram_tensor(f"in_{name}", a.shape, mybir.dt.from_np(a.dtype), kind="ExternalInput").ap()

    x = np.asarray(inputs["x"])
    put("xT", x.reshape(B, N, C).transpose(0, 2, 1).reshape(B, CH, P, N))
    put("consts", constants())
    l0 = {k[8:]: np.asarray(v) for k, v in inputs.items() if k.startswith("L0_conv_")}
    for name in ("w_in", "w_off", "w_mask", "b_in", "b_off", "b_mask"):
        put(name, l0[name])
    put("w_out0", l0["w_out"])
    by_channel = [l0[k] for k in ("dw_bias", "ln_gamma", "ln_beta", "b_out")]
    by_channel += [np.asarray(inputs[f"L3_conv_w{i}"]) for i in (1, 2, 3)]
    put("cols", np.stack(by_channel).reshape(7, CH, P).transpose(2, 0, 1))
    put("dwk", l0["dw_kernel"].reshape(K2, C).T)
    put("emb", inputs["L1_conv_embeddings"])
    put("embT", np.asarray(inputs["L1_conv_embeddings"]).T)
    put("w_qkv", inputs["L2_conv_w_qkv"])
    put("w_out2", inputs["L2_conv_w_out"])
    for i in (1, 2, 3):
        put(f"b{i}", inputs[f"L3_conv_b{i}"])
    out = nc.dram_tensor("out", (B, N, C), F32, kind="ExternalOutput").ap()
    build(nc, t, out)
    r = run(nc, [arrays], core_ids=[0])
    return r.results[0]["out"].reshape(B, H, W, C)
```
